# Optimizing a Trainium2 kernel written in Bass

```python
import numpy as np
import jax
import jax.numpy as jnp

def _softmax(x, axis=-1):
    return jax.nn.softmax(x, axis=axis)

def _gelu(x):
    return jax.nn.gelu(x, approximate=True)

def _silu(x):
    return jax.nn.silu(x)

def _sigmoid(x):
    return jax.nn.sigmoid(x)

def _layernorm(x, axis=-1, eps=1e-05):
    m = jnp.mean(x, axis=axis, keepdims=True)
    v = jnp.var(x, axis=axis, keepdims=True)
    return (x - m) / jnp.sqrt(v + eps)

def _scatter_add(tgt, idx, src, axis=0):
    return tgt.at[idx].add(src)

def _segment_sum(src, seg, n):
    return jax.ops.segment_sum(src, seg, n)
kernel_name = 'mk_gnn_resnorm_d4_gnn_r64_811cbc'

def setup_inputs(seed: int=0):
    np.random.seed(seed)
    _w = jnp.asarray

    def _rec_inputs():
        import jax
        import jax.numpy as jnp
        _gk = jax.random.key(seed)
        x = -0.0003713 + 1 * jax.random.normal(jax.random.fold_in(_gk, 1), (100000, 128), jnp.float32)
        src = jax.random.randint(jax.random.fold_in(_gk, 2), (50000,), 0, 100000, jnp.int32)
        dst = jax.random.randint(jax.random.fold_in(_gk, 3), (50000,), 0, 100000, jnp.int32)
        _o = jnp.argsort(dst, stable=True)
        src = src[_o]
        dst = dst[_o]
        edge_attr_48 = 5.93493e-05 + 1.00006 * jax.random.normal(jax.random.fold_in(_gk, 13), (50000, 48), jnp.float32)
        edge_weight = jax.random.uniform(jax.random.fold_in(_gk, 15), (50000,), jnp.float32, 0.0, 1)
        return (x, src, dst, edge_attr_48, edge_weight)
    x, src, dst, edge_attr_48, edge_weight = _rec_inputs()

    def _L0_gnn_setup():
        import jax, jax.numpy as jnp
        import numpy as np
        N_NODES = 100000
        N_EDGES = 50000
        IN_C = 128
        OUT_C = 128
        K = 3

        def _spmm(edge_row, edge_col, edge_vals, Z):
            msgs = edge_vals[:, None] * Z[edge_col]
            return jax.ops.segment_sum(msgs, edge_row, num_segments=N_NODES)
        key = jax.random.key(seed)
        k1, k2, k3, k4, k5, k6 = jax.random.split(key, 6)
        X = jax.random.normal(k1, (N_NODES, IN_C), dtype=jnp.float32)
        edge_row = jax.random.randint(k2, (N_EDGES,), 0, N_NODES, dtype=jnp.int32)
        edge_col = jax.random.randint(k3, (N_EDGES,), 0, N_NODES, dtype=jnp.int32)
        edge_vals = jax.random.uniform(k4, (N_EDGES,), dtype=jnp.float32)
        fan_in = (K + 1) * IN_C
        bound = 1.0 / np.sqrt(fan_in)
        W = jax.random.uniform(k5, (fan_in, OUT_C), dtype=jnp.float32, minval=-bound, maxval=bound)
        b = jax.random.uniform(k6, (OUT_C,), dtype=jnp.float32, minval=-bound, maxval=bound)
        return {'X': X, 'edge_row': edge_row, 'edge_col': edge_col, 'edge_vals': edge_vals, 'W': W, 'b': b}
    _L0_gnn_all = _L0_gnn_setup()
    _L0_gnn_in = {k: v for k, v in _L0_gnn_all.items() if k in ('W', 'b')}
    del _L0_gnn_all

    def _L1_gnn_setup():
        import jax, jax.numpy as jnp
        import numpy as np
        N, E, NODE_D, EDGE_D, GLOB_D, HID, B = (100000, 25000, 128, 48, 16, 256, 64)
        key = jax.random.key(seed)
        ks = jax.random.split(key, 9)
        x = jax.random.normal(ks[0], (N, NODE_D), dtype=jnp.float32)
        edge_index = jax.random.randint(ks[1], (2, E), 0, N, dtype=jnp.int32)
        edge_attr = jax.random.normal(ks[2], (E, EDGE_D), dtype=jnp.float32)
        u = jax.random.normal(ks[3], (B, GLOB_D), dtype=jnp.float32)
        batch = jnp.sort(jax.random.randint(ks[4], (N,), 0, B, dtype=jnp.int32))
        in_dim = NODE_D + 3 * EDGE_D + GLOB_D
        s1 = 1.0 / np.sqrt(in_dim)
        s2 = 1.0 / np.sqrt(HID)
        W1 = jax.random.uniform(ks[5], (in_dim, HID), jnp.float32, -s1, s1)
        b1 = jax.random.uniform(ks[6], (HID,), jnp.float32, -s1, s1)
        W2 = jax.random.uniform(ks[7], (HID, NODE_D), jnp.float32, -s2, s2)
        b2 = jax.random.uniform(ks[8], (NODE_D,), jnp.float32, -s2, s2)
        return {'x': x, 'edge_index': edge_index, 'edge_attr': edge_attr, 'u': u, 'batch': batch, 'W1': W1, 'b1': b1, 'W2': W2, 'b2': b2}
    _L1_gnn_all = _L1_gnn_setup()
    _L1_gnn_in = {k: v for k, v in _L1_gnn_all.items() if k in ('u', 'W1', 'b1', 'W2', 'b2')}
    del _L1_gnn_all

    def _L2_gnn_setup():
        import jax, jax.numpy as jnp
        import numpy as np
        N = 50000
        E = 12500
        D_IN = 128
        HEADS = 2
        C = 64
        key = jax.random.key(seed)
        ks = jax.random.split(key, 10)
        scale = 1.0 / np.sqrt(D_IN)
        x = jax.random.normal(ks[0], (N, D_IN), dtype=jnp.float32)
        edge_index = jax.random.randint(ks[1], (2, E), 0, N, dtype=jnp.int64)
        Wq = jax.random.normal(ks[2], (D_IN, HEADS * C), dtype=jnp.float32) * scale
        Wk = jax.random.normal(ks[3], (D_IN, HEADS * C), dtype=jnp.float32) * scale
        Wv = jax.random.normal(ks[4], (D_IN, HEADS * C), dtype=jnp.float32) * scale
        Wskip = jax.random.normal(ks[5], (D_IN, HEADS * C), dtype=jnp.float32) * scale
        bq = jnp.zeros((HEADS * C,), dtype=jnp.float32)
        bk = jnp.zeros((HEADS * C,), dtype=jnp.float32)
        bv = jnp.zeros((HEADS * C,), dtype=jnp.float32)
        bskip = jnp.zeros((HEADS * C,), dtype=jnp.float32)
        return {'x': x, 'edge_index': edge_index, 'Wq': Wq, 'bq': bq, 'Wk': Wk, 'bk': bk, 'Wv': Wv, 'bv': bv, 'Wskip': Wskip, 'bskip': bskip}
    _L2_gnn_all = _L2_gnn_setup()
    _L2_gnn_in = {k: v for k, v in _L2_gnn_all.items() if k in ('Wq', 'bq', 'Wk', 'bk', 'Wv', 'bv', 'Wskip', 'bskip')}
    del _L2_gnn_all

    def _L3_gnn_setup():
        import jax, jax.numpy as jnp
        import numpy as np
        N_NODES = 100000
        D = 128
        N_EDGES = 25000
        N_LAYERS = 3

        def _spmm(vals, rows, cols, x, n):
            gathered = vals[:, None] * x[cols]
            return jax.ops.segment_sum(gathered, rows, num_segments=n)
        key = jax.random.key(seed)
        k1, k2, k3, k4 = jax.random.split(key, 4)
        emb = jax.random.normal(k1, (N_NODES, D), dtype=jnp.float32)
        vals = jax.random.uniform(k2, (N_EDGES,), dtype=jnp.float32)
        rows = jax.random.randint(k3, (N_EDGES,), 0, N_NODES, dtype=jnp.int64 if jax.config.jax_enable_x64 else jnp.int32)
        cols = jax.random.randint(k4, (N_EDGES,), 0, N_NODES, dtype=jnp.int64 if jax.config.jax_enable_x64 else jnp.int32)
        return {'emb': emb, 'vals': vals, 'rows': rows, 'cols': cols}
    _L3_gnn_all = _L3_gnn_setup()
    _L3_gnn_in = {k: v for k, v in _L3_gnn_all.items() if k in ()}
    del _L3_gnn_all
    return {'x': x, 'src': src, 'dst': dst, 'edge_attr_48': edge_attr_48, 'edge_weight': edge_weight, 'L0_gnn_W': _L0_gnn_in['W'], 'L0_gnn_b': _L0_gnn_in['b'], 'L1_gnn_u': _L1_gnn_in['u'], 'L1_gnn_W1': _L1_gnn_in['W1'], 'L1_gnn_b1': _L1_gnn_in['b1'], 'L1_gnn_W2': _L1_gnn_in['W2'], 'L1_gnn_b2': _L1_gnn_in['b2'], 'L2_gnn_Wq': _L2_gnn_in['Wq'], 'L2_gnn_bq': _L2_gnn_in['bq'], 'L2_gnn_Wk': _L2_gnn_in['Wk'], 'L2_gnn_bk': _L2_gnn_in['bk'], 'L2_gnn_Wv': _L2_gnn_in['Wv'], 'L2_gnn_bv': _L2_gnn_in['bv'], 'L2_gnn_Wskip': _L2_gnn_in['Wskip'], 'L2_gnn_bskip': _L2_gnn_in['bskip']}

def reference(x, src, dst, edge_attr_48, edge_weight, L0_gnn_W, L0_gnn_b, L1_gnn_u, L1_gnn_W1, L1_gnn_b1, L1_gnn_W2, L1_gnn_b2, L2_gnn_Wq, L2_gnn_bq, L2_gnn_Wk, L2_gnn_bk, L2_gnn_Wv, L2_gnn_bv, L2_gnn_Wskip, L2_gnn_bskip):
    import jax
    import jax.numpy as jnp

    def _L0_gnn_ref(X, edge_row, edge_col, edge_vals, W, b):
        import jax, jax.numpy as jnp
        import numpy as np
        N_NODES = 100000
        N_EDGES = 50000
        IN_C = 128
        OUT_C = 128
        K = 3

        def _spmm(edge_row, edge_col, edge_vals, Z):
            msgs = edge_vals[:, None] * Z[edge_col]
            return jax.ops.segment_sum(msgs, edge_row, num_segments=N_NODES)
        Zs = [X]
        Z = X
        for _ in range(K):
            Z = _spmm(edge_row, edge_col, edge_vals, Z)
            Zs.append(Z)
        H = jnp.concatenate(Zs, axis=1)
        return H @ W + b

    def _L1_gnn_ref(x, edge_index, edge_attr, u, batch, W1, b1, W2, b2):
        import jax, jax.numpy as jnp
        import numpy as np
        N, E, NODE_D, EDGE_D, GLOB_D, HID, B = (100000, 25000, 128, 48, 16, 256, 64)
        col = edge_index[1]
        n = x.shape[0]
        out1 = jax.ops.segment_sum(edge_attr, col, num_segments=n)
        mx = jax.ops.segment_max(edge_attr, col, num_segments=n)
        cnt = jax.ops.segment_sum(jnp.ones((edge_attr.shape[0],), edge_attr.dtype), col, num_segments=n)
        has = (cnt > 0)[:, None]
        out2 = jnp.where(has, mx, 0.0)
        out3 = out1 / jnp.maximum(cnt, 1.0)[:, None]
        feat = jnp.concatenate([x, out1, out2, out3, u[batch]], axis=1)
        h = jax.nn.relu(feat @ W1 + b1)
        out = h @ W2 + b2
        return out + x

    def _L2_gnn_ref(x, edge_index, Wq, bq, Wk, bk, Wv, bv, Wskip, bskip):
        import jax, jax.numpy as jnp
        import numpy as np
        N = 50000
        E = 12500
        D_IN = 128
        HEADS = 2
        C = 64
        n = x.shape[0]
        src, dst = (edge_index[0], edge_index[1])
        q = (x @ Wq + bq).reshape(n, HEADS, C)
        k = (x @ Wk + bk).reshape(n, HEADS, C)
        v = (x @ Wv + bv).reshape(n, HEADS, C)
        alpha = (q[dst] * k[src]).sum(-1) * (1.0 / np.sqrt(C)).astype(np.float32)
        m = jax.ops.segment_max(alpha, dst, num_segments=n)
        a = jnp.exp(alpha - m[dst])
        denom = jax.ops.segment_sum(a, dst, num_segments=n)
        agg = jax.ops.segment_sum(a[:, :, None] * v[src], dst, num_segments=n)
        agg = agg / jnp.maximum(denom, 1e-16)[:, :, None]
        out = agg.reshape(n, HEADS * C) + (x @ Wskip + bskip)
        return out

    def _L3_gnn_ref(emb, vals, rows, cols):
        import jax, jax.numpy as jnp
        import numpy as np
        N_NODES = 100000
        D = 128
        N_EDGES = 25000
        N_LAYERS = 3

        def _spmm(vals, rows, cols, x, n):
            gathered = vals[:, None] * x[cols]
            return jax.ops.segment_sum(gathered, rows, num_segments=n)
        n = emb.shape[0]
        side = _spmm(vals, rows, cols, emb, n)
        light_out = (emb + N_LAYERS * side) / (N_LAYERS + 1)
        return light_out
    edge_index = jnp.stack([src, dst])
    batch0 = jnp.zeros((100000,), jnp.int32)
    x = _layernorm(x + _L0_gnn_ref(x, src, dst, edge_weight, L0_gnn_W, L0_gnn_b), axis=-1)
    x = _layernorm(x + _L1_gnn_ref(x, edge_index, edge_attr_48, L1_gnn_u, batch0, L1_gnn_W1, L1_gnn_b1, L1_gnn_W2, L1_gnn_b2), axis=-1)
    x = _layernorm(x + _L2_gnn_ref(x, edge_index, L2_gnn_Wq, L2_gnn_bq, L2_gnn_Wk, L2_gnn_bk, L2_gnn_Wv, L2_gnn_bv, L2_gnn_Wskip, L2_gnn_bskip), axis=-1)
    x = _layernorm(x + _L3_gnn_ref(x, edge_weight, src, dst), axis=-1)
    return x

_drawn_inputs = setup_inputs


def setup_inputs(seed=0):
    import zlib

    import numpy as np

    out = dict(_drawn_inputs(seed))
    spreads = {'L2_gnn_bq': (0.0, 0.8),
     'L2_gnn_bk': (0.0, 0.8),
     'L2_gnn_bv': (0.0, 0.1),
     'L2_gnn_bskip': (0.0, 0.1)}
    factors = {'L1_gnn_b1': 7.074, 'L1_gnn_b2': 2.897}
    for name, (base, spread) in spreads.items():
        noise = np.random.default_rng([zlib.crc32(name.encode()), seed]).standard_normal(out[name].shape)
        drawn = base * np.exp(spread * noise) if base else spread * noise
        out[name] = jnp.asarray(drawn.astype(out[name].dtype))
    for name, factor in factors.items():
        out[name] = (out[name] * factor).astype(out[name].dtype)
    return out
```

```python
from contextlib import ExitStack

import concourse.bass as bass
from concourse import mybir

F32 = mybir.dt.float32
BF16 = mybir.dt.bfloat16
I32 = mybir.dt.int32
I16 = mybir.dt.int16
ALU = mybir.AluOpType
ACT = mybir.ActivationFunctionType

P = 128
T = 4
G = T * P
EPS = 1e-5
FMAX = 3.4028234e38
BIG = 1 << 23
ZW = P + 4
DIG = 9
NB = 1 << DIG
ZC = 2048


def gnn_kernel(nc, x_fm, x_rows, src_g, dst_g, dnext_g, src_flat, dst_flat, w_flat, attr_fm,
               W0, b0, u, W1, b1, W2, b2, Wq, bq, Wk, bk, Wv, bv, Ws, bs, out):
    N_PAD, E_PAD = x_rows.shape[0], w_flat.shape[0]
    NI = N_PAD // (2 * G)
    EI = E_PAD // (2 * G)
    EC = E_PAD // P
    EB = EC // T
    AF = attr_fm.shape[0]
    AM = 64
    AK = AM + AF
    HID = W1.shape[1]
    HC = HID // P
    UF = u.shape[1]
    DPP = NI // 2
    TI = 2 * T
    assert NI == 2 * EI and DPP == EI and EB <= P and N_PAD <= NB * NB and AF <= AM

    ctx = ExitStack()
    with ctx:
        def sb(name, shape, dt=F32):
            return ctx.enter_context(nc.sbuf_tensor(name, shape, dt))

        def dram(name, shape, dt=F32):
            return nc.dram_tensor(name, shape, dt, kind="Internal").ap()

        AFTER = {
            "ld_last": ("ld_attr", EI * 80), "ld_x2d": ("ld_z", EI * 48), "st_x2d": ("st_zT", EI * 48),
            "qk": ("coded", EI), "maxed": ("numbered", EI), "decayed": ("ln1_out", NI + EI),
            "centred": ("attr_sums", EI), "delta": ("attr_mean", EI), "dmax": ("x2sel", EI), "rden": ("x2d", EI),
            "fin_scaled": ("weighted_v", EI), "fin_sum": ("agg", EI), "ld_z": ("ld_x", NI * 16),
            "q_mm": ("skip", NI + EI), "k_mm": ("x2_turned", NI + 2 * EI), "v_mm": ("hidden", NI + 2 * EI),
            "alpha": ("mlp", NI + 2 * EI), "skip_e": ("x1_turned", NI + 2 * EI), "agg_turned": ("mm1", NI + EI),
            "q_out": ("x1T", NI + 2 * EI), "decay": ("relu", NI + 2 * EI), "weight": ("x2T", NI + EI),
            "att_src": ("z_rows", 2 * EI),
        }

        def first_of(name):
            start = 0
            while name in AFTER:
                name, n = AFTER[name]
                start += n
            return name, start

        BASE = {n: first_of(n)[1] for n in AFTER}
        sems = {}

        def S(name, s=""):
            key = f"{first_of(name)[0]}{s}"
            if key not in sems:
                sems[key] = ctx.enter_context(nc.semaphore(key))
            return sems[key]

        Z1N = dram("Z1N", [N_PAD, ZW])
        Z2E = dram("Z2E", [E_PAD + 1, P])
        XT = dram("XT", [N_PAD, 3 * P])
        XT3 = XT.rearrange("n (k f) -> (n k) f", k=3)
        ZT = [dram(f"Z{k}T", [P, E_PAD]) for k in (1, 2, 3)]
        ATT = dram("ATT", [AK, E_PAD])
        MNT = dram("MNT", [AF, E_PAD])
        X2DT = dram("X2DT", [P, E_PAD])
        ROWS = {n: dram(f"row_{n}", [1, E_PAD]) for n in ("same", "samem", "notlast", "last", "inv", "s_same", "s_w")}
        TAB = {n: dram(f"tab_{n}", [EC // T, P, T], I32) for n in (
            "d_x1", "d_x2_out", "d_x3_out", "d_out",
            "d_x2s",
            "s_dst", "s_src", "s_out",
            "s_x3d", "s_x3s", "s_z")}
        PAY = dram("PAY", [E_PAD + 2, 4], I32)
        PLOW = dram("PLOW", [E_PAD + 2, 4], I32)
        PSRC = dram("PSRC", [E_PAD + 2, 4], I32)
        cols_d = dram("cols_d", [3, P])

        bank = [ctx.enter_context(nc.psum_tensor(f"bank{b}", [P, T, P], F32)) for b in range(8)]
        bT1, bTR, bH0, bH1, bMLP, bSK, bIN, bBK = bank
        bH = [bH0, bH1]

        ident = sb("ident", [P, P])
        W0I = sb("W0I", [P, 4, P])
        W1x = sb("W1x", [P, HID])
        W1a = sb("W1a", [P, HID])
        W1m = sb("W1m", [P, HID])
        W1u = sb("W1u", [UF, HID])
        ucol = sb("ucol", [UF, 1])
        b1c = sb("b1c", [P, HC])
        b1u = sb("b1u", [P, HC])
        W2s = sb("W2s", [P, HC, P])
        Wqs, Wks, Wvs = sb("Wqs", [P, P]), sb("Wks", [P, P]), sb("Wvs", [P, P])
        bqc, bkc, bvc = sb("bqc", [P, 1]), sb("bkc", [P, 1]), sb("bvc", [P, 1])
        WsI = sb("WsI", [P, P])
        heads = sb("heads", [P, P])
        hsel = sb("hsel", [P, 2])
        epsc = sb("epsc", [P, 1])
        ones3 = sb("ones3", [3, P], BF16)
        brow = sb("brow", [1, 3, P])
        bres = sb("bres", [1, 3, P])
        bres2 = sb("bres2", [1, 3, P])
        bsp = sb("bsp", [1, 3, 3, P], BF16)
        bias3 = sb("bias3", [3, 3, P], BF16)
        zeros = sb("zeros", [P, ZC])
        hzero = zeros[:, 0:NB]

        tabs = {"s_z": sb("t_s_z", [P, EC], I32)}
        enum = sb("enum", [P, EC])
        codes = sb("codes", [P, EC])
        idx, idx2, sct = ([sb(f"{n}{s}", [P, T], I32) for s in range(2)] for n in ("idx", "idx2_", "sct"))

        prep_ctx = ExitStack()

        def early(name, shape, dt=F32):
            return prep_ctx.enter_context(nc.sbuf_tensor(name, shape, dt))

        dstp, dstc, dstn = early("dstp", [P, EC], I32), early("dstc", [P, EC], I32), early("dstn", [P, EC], I32)
        same, samem = early("same", [P, EC]), early("samem", [P, EC])
        notlast, last = early("notlast", [P, EC]), early("last", [P, EC])
        onesE = early("onesE", [P, EC])
        cntl, allsame, inv = early("cntl", [P, EC]), early("allsame", [P, EC]), early("inv", [P, EC])
        crow = early("crow", [1, 3, P])
        ccol = early("ccol", [P, 1])
        gdst, gdn = early("gdst", [P, EC], I32), early("gdn", [P, EC], I32)
        gsrc, geq = early("gsrc", [P, EC], I32), early("geq", [P, EC])
        tabs.update((n, early(f"t_{n}", [P, EC], I32)) for n in TAB if n != "s_z")
        enum_i = early("enum_i", [P, EC], I32)
        ctmp, ctmp2 = early("ctmp", [P, EC]), early("ctmp2", [P, EC])
        fsrc, fdst, fw = early("fsrc", [P, EC], I32), early("fdst", [P, EC], I32), early("fw", [P, EC])
        payl = early("payl", [P, EC, 4], I32)
        digi = early("digi", [P, 2, EC], I32)
        digf = early("digf", [P, 2, EC])
        buckets_i, buckets = early("buckets_i", [P, NB], I32), early("buckets", [P, NB], I16)
        oh = [early(f"oh{r}", [P, NB], BF16) for r in range(4)]
        ohh = [early(f"ohh{r}", [P, NB], BF16) for r in range(4)]
        before, rest, ones = early("before", [P, P], BF16), early("rest", [P, P], BF16), early("ones", [P, P], BF16)
        hscan, base = early("hscan", [P, 2, NB]), early("base", [P, 2, NB])
        junk = [early(f"junk{r}", [P, NB]) for r in range(2)]
        minus = early("minus", [1, 4], I32)
        pb = [early(f"pb{o}", [EB, T, P, 4], I32) for o in range(3)]
        bsame, bw, bsrc, bdst, bout = (early(n, [EB, T, P]) for n in ("bsame", "bw", "bsrc", "bdst", "bout"))

        pay = [early(f"pay{s}", [P, T, 4], I32) for s in range(2)]
        dig4i = [early(f"dig4i{s}", [P, T], I32) for s in range(2)]
        dig4 = [early(f"dig4_{s}", [P, T]) for s in range(2)]
        pos4 = [early(f"pos4_{s}", [P, T]) for s in range(2)]
        prep_ctx.close()

        def two(name, shape, dt=F32):
            return [sb(f"{name}{s}", shape, dt) for s in range(2)]

        own = two("own", [P, T, P])
        gat = two("gat", [P, T, ZW])
        fB, wB, fmB, invB, f2B = (two(n, [P, G]) for n in ("fB", "wB", "fmB", "invB", "f2B"))
        msg, zT = two("msg", [P, G]), two("zT", [P, G])
        zE = two("zE", [P, T, ZW])
        atr = two("atr", [P, G])
        att = two("att", [P, G])
        mnt = two("mnt", [AF, G])
        xT = two("xT", [P, T, P])
        xc = two("xc", [P, T, 3, P])
        x1, x2, x3 = ([c[:, :, k, :] for c in xc] for k in range(3))
        x1T = two("x1T", [P, G])
        hT = [two(f"hT{c}_", [P, G]) for c in range(HC)]
        t2, x2T, x4 = two("t2", [P, T, P]), two("x2T", [P, T, P]), two("x4", [P, T, P])
        zin = [two(f"zin{k}_", [P, T, P]) for k in range(3)]
        x2d = two("x2d", [P, G])
        mbuf = two("mbuf", [P, G + 1])
        ln = {}
        for n in ("ln1", "ln2", "ln3", "ln4"):
            ln[n] = (two(n + "st", [P, T, 6]), two(n + "mv", [P, T, 2]), two(n + "sd", [P, T]), two(n + "rs", [P, T]))
        lns = {(c, k): ln[f"ln{k + 1}"] for c, ks in (("node", range(4)), ("s", range(3)), ("d", (1,)),
                                                      ("att", (2, 3)), ("fin", (3,))) for k in ks}
        rden = two("rden", [P, 2 * T])
        dmax = two("dmax", [P, 2 * T])

        def flat(t):
            return t[:, :, :].rearrange("p t f -> p (t f)")

        mnt_w = wB
        xs, qT, prod, dlt, dec, elt, aw, av, den, agg, aggn = (
            x1T, hT[0], hT[1], [flat(a) for a in zin[0]], [flat(a) for a in zin[1]], [flat(a) for a in zin[2]],
            mnt_w, atr, att, msg, x2T)

        def epos(g):
            return bass.ds(g * G, G)

        def at(eng, name, s, count):
            count = count + BASE.get(name, 0)
            if isinstance(count, int) and count <= 0:
                return
            eng.wait_ge(S(name, s), count)
            if eng.engine == mybir.EngineType.SP:
                eng.sem_inc(S("go_sp"), 1)

        def ready(eng, name, s, i, n=1):
            at(eng, name, s, (i + 1) * n)

        def reuse(eng, name, s, i, n=1):
            at(eng, name, s, i * n)

        def prior(eng, name, s, i, n=1):
            if s == 1:
                at(eng, name, 0, (i + 1) * n)
            else:
                at(eng, name, 1, i * n)

        def prepared(eng):
            eng.wait_ge(S("st_rows"), 16 * 7)
            eng.wait_ge(S("st_tab"), 16 * 10)

        def repeated(eng, n):
            def run(body):
                body(0)
                with eng.Fori(1, n) as i:
                    body(i)
            return run

        block = ctx.enter_context(nc.Block())
        ctx.enter_context(nc.allow_non_contiguous_dma(reason="index tables of four words per partition"))

        def seq(k, i):
            return i + k * EI

        def ci(kind, i):
            return i + {"node": 0, "s": NI, "d": NI + EI}[kind]

        def norms(where, k, i):
            first, each, start = {"node": (0, 4, 0), "s": (0, 3, 4 * NI), "d": (1, 1, 4 * NI + 3 * EI),
                                  "att": (2, 2, 4 * NI + 4 * EI), "fin": (3, 1, 4 * NI + 6 * EI)}[where]
            return i * each + (start + k - first + 1)

        def tile_no(k, i, j):
            return i * TI + (k * EC + j)

        def tiles_done(eng, name, count):
            if isinstance(count, int) and count <= 0:
                return
            eng.wait_ge(S(name), count)

        @block.sync
        def _(sp):
            def table_store(name, n=16):
                sp.dma_start(TAB[name].rearrange("g p t -> p g t"),
                             tabs[name][:, :].rearrange("p (g t) -> p g t", t=T)).then_inc(S("st_tab"), n)

            for t, a in ((fsrc, src_flat), (fdst, dst_flat[1:E_PAD + 1]), (fw, w_flat)):
                sp.dma_start(t[:, :], a.rearrange("(p c) -> p c", p=P)).then_inc(S("ld_flat"), 16)
            sp.dma_start(gsrc[:, :].rearrange("p (g t) -> p g t", t=T), src_g.rearrange("g p t -> p g t")
                         ).then_inc(S("ld_gsrc"), 16)
            sp.dma_start(dstp[:, :], dst_flat[0:E_PAD].rearrange("(p c) -> p c", p=P)).then_inc(S("ld_prep"), 16)
            sp.dma_start(dstc[:, :], dst_flat[1:E_PAD + 1].rearrange("(p c) -> p c", p=P)).then_inc(S("ld_prep"), 16)
            sp.dma_start(dstn[:, :], dst_flat[2:E_PAD + 2].rearrange("(p c) -> p c", p=P)).then_inc(S("ld_prep"), 16)
            for t, a in ((gdst, dst_g), (gdn, dnext_g)):
                sp.dma_start(t[:, :].rearrange("p (g t) -> p g t", t=T),
                             a.rearrange("g p t -> p g t")).then_inc(S("ld_prep"), 16)
            for t, a in ((W0I[:, :, :], W0.rearrange("(k p) n -> p k n", p=P)),
                         (W1x[:, :], W1[0:P, :]),
                         (W1u[:, :], W1[P + 3 * AF:P + 3 * AF + UF, :]),
                         (ucol[:, :], u[0:1, :].rearrange("a f -> f a")),
                         (b1c[:, :], b1.rearrange("(c p) -> p c", p=P)),
                         (W2s[:, :, :], W2.rearrange("(c p) n -> p c n", p=P)),
                         (Wqs[:, :], Wq), (Wks[:, :], Wk), (Wvs[:, :], Wv), (WsI[:, :], Ws),
                         (bqc[:, :], bq.rearrange("(p a) -> p a", a=1)),
                         (bkc[:, :], bk.rearrange("(p a) -> p a", a=1)),
                         (bvc[:, :], bv.rearrange("(p a) -> p a", a=1)),
                         (brow[:, 0, :], b0.rearrange("(a p) -> a p", a=1)),
                         (brow[:, 1, :], b2.rearrange("(a p) -> a p", a=1)),
                         (brow[:, 2, :], bs.rearrange("(a p) -> a p", a=1))):
                sp.dma_start(t, a).then_inc(S("ld_const"), 16)
            sp.wait_ge(S("init_w1"), 1)
            for t, a in ((W1a[0:AF, :], W1[P:P + AF, :]),
                         (W1a[AM:AK, :], W1[P + AF:P + 2 * AF, :]),
                         (W1m[0:AF, :], W1[P + 2 * AF:P + 3 * AF, :])):
                sp.dma_start(t, a).then_inc(S("ld_const"), 16)
            sp.wait_ge(S("payload"), 3)
            sp.dma_start(PAY[1:E_PAD + 1, :].rearrange("(p c) w -> p (c w)", p=P),
                         payl[:, :, :].rearrange("p c w -> p (c w)")).then_inc(S("st_pay"), 16)
            sp.wait_ge(S("minus"), 1)
            for r in (0, E_PAD + 1):
                sp.dma_start(PSRC[r:r + 1, :], minus[:, :]).then_inc(S("st_pay"), 16)
            sp.wait_ge(S("init_zero"), 1)
            zflat = Z1N.rearrange("(p a) w -> p (a w)", p=P)
            n = zflat.shape[1]
            for a in range(0, n, ZC):
                m = min(ZC, n - a)
                sp.dma_start(zflat[:, a:a + m], zeros[:, 0:m]).then_inc(S("zeroed"), 16)
            sp.dma_start(Z2E[0:1, :], zeros[0:1, 0:P]).then_inc(S("zeroed"), 16)
            sp.wait_ge(S("cnt_local"), 2)
            sp.dma_start(cols_d[0:1, :].rearrange("a p -> p a"), cntl[:, EC - 1:EC]).then_inc(S("carry"), 16)
            sp.dma_start(cols_d[1:2, :].rearrange("a p -> p a"), allsame[:, EC - 1:EC]).then_inc(S("carry"), 16)
            sp.wait_ge(S("carry"), 32)
            sp.dma_start(crow[:, 0:2, :], cols_d[0:2, :].rearrange("(o a) p -> o a p", o=1)).then_inc(S("carry_row"), 16)
            sp.wait_ge(S("carry_scan"), 1)
            sp.dma_start(cols_d[2:3, 1:P], crow[0:1, 2, 0:P - 1]).then_inc(S("carry_out"), 16)
            sp.dma_start(cols_d[2:3, 0:1], zeros[0:1, 0:1]).then_inc(S("carry_out"), 16)
            sp.wait_ge(S("carry_out"), 32)
            sp.dma_start(ccol[:, :], cols_d[2:3, :].rearrange("a p -> p a")).then_inc(S("carry_col"), 16)
            sp.wait_ge(S("flags"), 1)
            for nm, t in (("same", same), ("samem", samem), ("notlast", notlast), ("last", last)):
                sp.dma_start(ROWS[nm].rearrange("a (p c) -> (a p) c", p=P), t[:, :]).then_inc(S("st_rows"), 16)
            sp.wait_ge(S("inv"), 1)
            sp.dma_start(ROWS["inv"].rearrange("a (p c) -> (a p) c", p=P), inv[:, :]).then_inc(S("st_rows"), 16)
            sp.wait_ge(S("d_tabs"), 6)
            for nm in ("d_x1", "d_x2_out", "d_x3_out", "d_out", "d_x2s"):
                table_store(nm)
            sp.wait_ge(S("bias_split"), 3)
            for k in range(3):
                sp.dma_start(bias3[k:k + 1, :, :], bsp[0:1, k, :, :]).then_inc(S("ld_bias"), 16)

            sp.wait_ge(S("st_pay"), 48)
            for k in (1, 2):
                table = {1: PAY, 2: PLOW}[k]
                if k == 2:
                    for s in range(2):
                        at(sp, "placed", s, EI * 64)

                def pay_loads(i):
                    for s in range(2):
                        at(sp, "placed", s, i * 64 + (k - 1) * EI * 64)
                        sp.dma_start(pay[s][:, :, :], table[bass.ds((i * 2 + s) * G + 1, G), :]
                                     .rearrange("(t p) w -> p t w", p=P)).then_inc(S("ld_pay", s), 16)

                pay_loads(0)
                with sp.Fori(1, EI) as i:
                    pay_loads(i)

            for s in range(2):
                at(sp, "placed", s, 2 * EI * 64)
            for o in range(3):
                sp.dma_start(pb[o][:, :, :, :].rearrange("p b n w -> p b (n w)"),
                             PSRC[o:o + E_PAD, :].rearrange("(b p n) w -> p b (n w)", b=T, p=EB)
                             ).then_inc(S("ld_blocks"), 16)
            sp.wait_ge(S("s_rows"), 2)
            for nm, t in (("s_same", bsame), ("s_w", bw)):
                sp.dma_start(ROWS[nm].rearrange("a (b p n) -> p (a b) n", b=T, p=EB), t[:, :, :]
                             ).then_inc(S("st_rows"), 16)
            sp.wait_ge(S("s_tabs"), 5)
            for nm in ("s_dst", "s_src", "s_out", "s_x3d", "s_x3s"):
                table_store(nm)
            prepared(sp)

            def row_load(t, row, g, sem):
                sp.dma_start(t[:, :], row[0:1, epos(g)].to_broadcast([P, G])).then_inc(sem, 16)

            def index_load(t, name, g, sem):
                sp.dma_start(t[:, :], TAB[name][bass.ds(g, 1)].rearrange("g p t -> (g p) t")).then_inc(sem, 16)

            def gather_index(k, i, name):
                for s in range(2):
                    at(sp, "gathered", s, seq(k, i) * 64)
                    index_load(idx[s], name, i * 2 + s, S("ld_idx", s))

            def scatter_index(k, i, name, rev=False):
                for s in range(2):
                    at(sp, "scattered", s, seq(k, i) * 64)
                    index_load(sct[s], name, edge_group(i, s, rev), S("ld_sct", s))

            def edge_group(i, s, rev):
                return (2 * EI - 1 - s) - i * 2 if rev else i * 2 + s

            def spmm_rows(k, i):
                for s in range(2):
                    at(sp, "scanned", s, seq(k, i))
                    row_load(fB[s], ROWS["s_same"], i * 2 + s, S("ld_row", s))
                    row_load(wB[s], ROWS["s_w"], i * 2 + s, S("ld_row", s))

            def z_loads(k, i):
                gather_index(k, i, ("s_dst", "s_dst", "s_z")[k])
                spmm_rows(k, i)
                if k == 0:
                    scatter_index(0, i, "s_out")

            def z_stores(k, i):
                for s in range(2):
                    g = i * 2 + s
                    ready(sp, "scanned", s, seq(k, i))
                    sp.dma_start(ZT[k][:, epos(g)], zT[s][:, :]).then_inc(S("st_zT", s), 16)
                    if k == 1:
                        ready(sp, "z_rows", s, seq(1, i))
                        sp.dma_start(Z2E[bass.ds(g * G + 1, G), :].rearrange("(t p) f -> p t f", p=P),
                                     zE[s][:, :, 0:P]).then_inc(S("st_z2", s), 16)

            def node_loads(i):
                for s in range(2):
                    reuse(sp, "mm1", s, i)
                    sp.dma_start(flat(xT[s]), x_fm[:, bass.ds((i * 2 + s) * G, G)]).then_inc(S("ld_x", s), 16)

            def rows_of(table, g):
                return table[bass.ds(g * G, G), :].rearrange("(p t) f -> p t f", t=T)

            def node_stores(i):
                for s in range(2):
                    ready(sp, "ln3_out", s, i)
                    sp.dma_start(XT[bass.ds((i * 2 + s) * G, G), :].rearrange("(p t) f -> p (t f)", t=T),
                                 xc[s][:, :, :, :].rearrange("p t k f -> p (t k f)")).then_inc(S("st_xt", s), 16)
                for s in range(2):
                    ready(sp, "ln4_out", s, i)
                    sp.dma_start(rows_of(out, i * 2 + s), x4[s][:, :, :]).then_inc(S("st_x4", s), 16)

            for k in range(2):
                z_loads(k, 0)
                node_loads(DPP * k)
                with sp.Fori(1, EI) as i:
                    z_loads(k, i)
                    node_loads(i + DPP * k)
                    z_stores(k, i - 1)
                    node_stores(i + (DPP * k - 1))
                z_stores(k, EI - 1)
                node_stores(DPP * k + EI - 1)

            sp.wait_ge(S("s_ztab"), 1)
            table_store("s_z")
            sp.wait_ge(S("st_tab"), 16 * 11)

            def attr_loads(i):
                for s in range(2):
                    g = i * 2 + s
                    reuse(sp, "attr_mean", s, i)
                    for p0 in (0, AM):
                        sp.dma_start(atr[s][p0:p0 + AF, :], attr_fm[:, epos(g)]).then_inc(S("ld_attr", s), 16)
                    row_load(f2B[s], ROWS["same"], g, S("ld_attr", s))
                    row_load(fmB[s], ROWS["samem"], g, S("ld_attr", s))
                    row_load(invB[s], ROWS["inv"], g, S("ld_attr", s))

            def attr_stores(i):
                for s in range(2):
                    g = i * 2 + s
                    ready(sp, "attr_mean", s, i)
                    sp.dma_start(ATT[:, epos(g)], att[s][0:AK, :]).then_inc(S("st_att", s), 16)
                    sp.dma_start(MNT[:, epos(g)], mnt[s][:, :]).then_inc(S("st_att", s), 16)

            z_loads(2, 0)
            attr_loads(0)
            with sp.Fori(1, EI) as i:
                z_loads(2, i)
                attr_loads(i)
                z_stores(2, i - 1)
                attr_stores(i - 1)
            z_stores(2, EI - 1)
            attr_stores(EI - 1)

            for s in range(2):
                at(sp, "st_zT", s, 3 * EI * 16)

            def source_loads(i):
                gather_index(3, i, "s_src")
                scatter_index(1, i, "s_out")
                for s in range(2):
                    reuse(sp, "mm1", s, ci("s", i))
                    for k in range(3):
                        sp.dma_start(flat(zin[k][s]), ZT[k][:, epos(i * 2 + s)]).then_inc(S("ld_z", s), 16)

            source_loads(0)
            with sp.Fori(1, EI) as i:
                source_loads(i)

            for s in range(2):
                at(sp, "st_att", s, EI * 32)

            def dst_loads(i):
                for s in range(2):
                    at(sp, "gathered", s, seq(4, i) * 64)
                    index_load(idx[s], "d_x1", edge_group(i, s, True), S("ld_idx", s))
                scatter_index(2, i, "d_x2_out", rev=True)
                for s in range(2):
                    g = edge_group(i, s, True)
                    reuse(sp, "hidden", s, ci("d", i))
                    sp.dma_start(att[s][0:AK, :], ATT[:, epos(g)]).then_inc(S("ld_att", s), 16)
                    sp.dma_start(mnt[s][:, :], MNT[:, epos(g)]).then_inc(S("ld_att", s), 16)
                    reuse(sp, "x2d", s, i)
                    row_load(f2B[s], ROWS["last"], g, S("ld_last", s))
                    row_load(fmB[s], ROWS["notlast"], g, S("ld_last", s))

            def dst_stores(i):
                for s in range(2):
                    ready(sp, "x2d", s, i)
                    sp.dma_start(X2DT[:, epos(edge_group(i, s, True))], x2d[s][:, :]).then_inc(S("st_x2d", s), 16)

            dst_loads(0)
            with sp.Fori(1, EI) as i:
                dst_loads(i)
                dst_stores(i - 1)
            dst_stores(EI - 1)

            for s in range(2):
                at(sp, "st_x2d", s, 16 * EI)

            def att_loads(i):
                gather_index(5, i, "d_x2s")
                scatter_index(3, i, "d_x3_out")
                for s in range(2):
                    reuse(sp, "scattered2", s, i, 64)
                    index_load(idx2[s], "d_out", i * 2 + s, S("ld_idx2", s))
                for s in range(2):
                    g = i * 2 + s
                    reuse(sp, "skip_e", s, i)
                    reuse(sp, "decayed", s, i)
                    sp.dma_start(x2d[s][:, :], X2DT[:, epos(g)]).then_inc(S("ld_x2d", s), 16)
                    row_load(fmB[s], ROWS["samem"], g, S("ld_x2d", s))

            att_loads(0)
            with sp.Fori(1, EI) as i:
                att_loads(i)

            def fin_loads(i):
                gather_index(6, i, "s_x3d")
                spmm_rows(3, i)
                for s in range(2):
                    if isinstance(i, int) and i == 0:
                        at(sp, "scattered2", s, EI * 64)
                    reuse(sp, "gathered2", s, i, 64)
                    index_load(idx2[s], "s_x3s", i * 2 + s, S("ld_idx2", s))
                scatter_index(4, i, "s_out")

            for s in range(2):
                at(sp, "agg", s, EI)
                at(sp, "weighted_v", s, EI)
            fin_loads(0)
            with sp.Fori(1, EI) as i:
                fin_loads(i)

        @block.gpsimd
        def _(pool):
            pool.iota(enum_i[:, :], pattern=[[P, EC]], base=1, channel_multiplier=1).then_inc(S("enum_i"), 1)
            pool.memset(ident[:, :], 0.0).then_inc(S("ident0"), 1)
            pool.wait_ge(S("ident0"), 1)
            pool.affine_select(out=ident[:, :], in_=ident[:, :], compare_op=ALU.not_equal, fill=1.0, base=0,
                               pattern=[[-1, P]], channel_multiplier=1).then_inc(S("ident"), 1)

            pool.iota(buckets_i[:, :], pattern=[[1, NB]], base=0, channel_multiplier=0).then_inc(S("enum_i"), 1)
            pool.memset(before[:, :], 1.0).then_inc(S("ident0"), 1)
            pool.memset(rest[:, :], 1.0).then_inc(S("ident0"), 1)
            pool.memset(ones[:, :], 1.0).then_inc(S("ident0"), 1)
            pool.memset(minus[:, :], -1).then_inc(S("minus"), 1)
            pool.wait_ge(S("ident0"), 4)
            pool.affine_select(out=before[:, :], in_=before[:, :], compare_op=ALU.is_gt, fill=0.0, base=0,
                               pattern=[[1, P]], channel_multiplier=-1).then_inc(S("triangles"), 1)
            pool.affine_select(out=rest[:, :], in_=rest[:, :], compare_op=ALU.is_ge, fill=0.0, base=0,
                               pattern=[[-1, P]], channel_multiplier=1).then_inc(S("triangles"), 1)

            def gather(table, width, tile, index, sem):
                pool.sem_inc(S("go"), 1)
                for t in range(T):
                    pool.indirect_dma_start(
                        out=tile[:, t, 0:width], out_offset=None, in_=table,
                        in_offset=bass.IndirectOffsetOnAxis(ap=index[:, t:t + 1], axis=0)).then_inc(sem, 16)

            def scatter(table, rows, index, sem):
                pool.sem_inc(S("go"), 1)
                for t in range(T):
                    pool.indirect_dma_start(
                        out=table, out_offset=bass.IndirectOffsetOnAxis(ap=index[:, t:t + 1], axis=0),
                        in_=rows[t], in_offset=None,
                        bounds_check=table.shape[0] - 1, oob_is_err=False).then_inc(sem, 16)

            for k in (1, 2):
                @repeated(pool, EI)
                def _(i):
                    for s in range(2):
                        at(pool, "ranked", s, i + ((k - 1) * EI + 1))
                        scatter(PLOW if k == 1 else PSRC, [pay[s][:, t, :] for t in range(T)], idx[s],
                                S("placed", s))

            prepared(pool)

            def z_gather(k, i):
                table = [x_rows, Z1N, Z2E][k]
                for s in range(2):
                    at(pool, "turned", s, seq(k, i))
                    if k == 1:
                        reuse(pool, "coded", s, i)
                    ready(pool, "ld_idx", s, seq(k, i), 16)
                    gather(table, ZW if k == 1 else P, gat[s], idx[s], S("gathered", s))

            def z_scatter(i):
                for s in range(2):
                    ready(pool, "ld_sct", s, i, 16)
                    ready(pool, "z_rows", s, i)
                    ready(pool, "numbered", s, i)
                    scatter(Z1N, [zE[s][:, t, :] for t in range(T)], sct[s], S("scattered", s))

            z_gather(0, 0)
            pool.wait_ge(S("zeroed"), 16 * ((N_PAD * ZW // P + ZC - 1) // ZC + 1))
            with pool.Fori(1, EI) as i:
                z_gather(0, i)
                z_scatter(i - 1)
            z_scatter(EI - 1)
            for s in range(2):
                at(pool, "scattered", s, EI * 64)

            @repeated(pool, EI)
            def _(i):
                z_gather(1, i)
            for s in range(2):
                at(pool, "st_z2", s, EI * 16)
                at(pool, "coded", s, EI)

            @repeated(pool, EI)
            def _(i):
                z_gather(2, i)

            def source_gather(i):
                for s in range(2):
                    at(pool, "turned", s, seq(3, i))
                    ready(pool, "ld_idx", s, seq(3, i), 16)
                    gather(x_rows, P, gat[s], idx[s], S("gathered", s))

            def source_scatter(i):
                for s in range(2):
                    ready(pool, "ld_sct", s, seq(1, i), 16)
                    ready(pool, "ln3_out", s, ci("s", i))
                    scatter(XT, [xc[s][:, t, :, :].rearrange("p k f -> p (k f)") for t in range(T)], sct[s],
                            S("scattered", s))

            for s in range(2):
                at(pool, "st_xt", s, NI * 16)
            source_gather(0)
            with pool.Fori(1, EI) as i:
                source_gather(i)
                source_scatter(i - 1)
            source_scatter(EI - 1)

            for s in range(2):
                at(pool, "scattered", s, 2 * EI * 64)
                at(pool, "turned", s, 4 * EI)

            def dst_gather(i):
                for s in range(2):
                    if not isinstance(i, int) or i > 0:
                        at(pool, "x1_turned", s, ci("d", i))
                        at(pool, "t2", s, ci("d", i))
                    ready(pool, "ld_idx", s, seq(4, i), 16)
                    gather(XT3, P, gat[s], idx[s], S("gathered", s))

            def dst_scatter(i):
                for s in range(2):
                    ready(pool, "ld_sct", s, seq(2, i), 16)
                    ready(pool, "ln2_out", s, ci("d", i))
                    scatter(XT3, [x2[s][:, t, :] for t in range(T)], sct[s], S("scattered", s))

            dst_gather(0)
            with pool.Fori(1, EI) as i:
                dst_gather(i)
                dst_scatter(i - 1)
            dst_scatter(EI - 1)

            for s in range(2):
                at(pool, "scattered", s, 3 * EI * 64)
                at(pool, "x1_turned", s, NI + 2 * EI)
                at(pool, "t2", s, NI + 2 * EI)
                at(pool, "st_x4", s, 16 * NI)

            def att_gather(i):
                for s in range(2):
                    at(pool, "turned", s, seq(4, i))
                    ready(pool, "ld_idx", s, seq(5, i), 16)
                    gather(XT3, P, gat[s], idx[s], S("gathered", s))

            def att_scatter(i):
                for s in range(2):
                    ready(pool, "ld_sct", s, seq(3, i), 16)
                    ready(pool, "ln3_out", s, i + NI + EI)
                    scatter(XT3, [x3[s][:, t, :] for t in range(T)], sct[s], S("scattered", s))
                for s in range(2):
                    ready(pool, "ld_idx2", s, i, 16)
                    ready(pool, "ln4_out", s, i + NI)
                    scatter(out, [x4[s][:, t, :] for t in range(T)], idx2[s], S("scattered2", s))

            att_gather(0)
            with pool.Fori(1, EI) as i:
                att_gather(i)
                att_scatter(i - 1)
            att_scatter(EI - 1)

            for s in range(2):
                at(pool, "scattered", s, 4 * EI * 64)
                at(pool, "scattered2", s, EI * 64)

            def fin_gather(i):
                for s in range(2):
                    at(pool, "turned", s, seq(5, i))
                    ready(pool, "ld_idx", s, seq(6, i), 16)
                    gather(XT3, P, gat[s], idx[s], S("gathered", s))
                    reuse(pool, "fin_scaled", s, i)
                    ready(pool, "ld_idx2", s, seq(1, i), 16)
                    gather(XT3, P, own[s], idx2[s], S("gathered2", s))

            def fin_scatter(i):
                for s in range(2):
                    ready(pool, "ld_sct", s, seq(4, i), 16)
                    ready(pool, "ln4_out", s, i + NI + EI)
                    scatter(out, [x4[s][:, t, :] for t in range(T)], sct[s], S("scattered", s))

            fin_gather(0)
            with pool.Fori(1, EI) as i:
                fin_gather(i)
                fin_scatter(i - 1)
            fin_scatter(EI - 1)
            for s in range(2):
                at(pool, "scattered", s, 5 * EI * 64)

        @block.tensor
        def _(pe):
            pe.wait_ge(S("ident"), 1)
            pe.wait_ge(S("triangles"), 2)

            bLOW, bHIGH = bT1, bTR

            @repeated(pe, EI)
            def _(i):
                for j in range(TI):
                    first = isinstance(i, int) and i + j == 0
                    tiles_done(pe, "one_hot", tile_no(0, i, j + 1))
                    pe.matmul(bLOW[:, :, :], ones[:, :], oh[j % 4][:, :], start=first, stop=False, skip_group_check=True)
                    pe.matmul(bHIGH[:, :, :], ones[:, :], ohh[j % 4][:, :], start=first, stop=False,
                              skip_group_check=True).then_inc(S("counted"), 1)

            for k in (1, 2):
                pair = (bH0, bH1) if k == 1 else (bMLP, bSK)
                pe.wait_ge(S("bases"), 2)
                for b in range(2):
                    pe.matmul(pair[b][:, :, :], ident[:, :], base[:, k - 1, :], start=True, stop=False,
                              skip_group_check=True)

                @repeated(pe, EI)
                def _(i):
                    for j in range(TI):
                        bk_ = pair[j % 2]
                        first = isinstance(i, int) and i == 0
                        tiles_done(pe, "one_hot", tile_no(k, i, j + 1))
                        if not first or j >= 2:
                            tiles_done(pe, "ranked_tile", tile_no(k - 1, i, j - 1))
                            pe.matmul(bk_[:, :, :], rest[:, :], oh[(j - 2) % 4][:, :], start=False, stop=False,
                                      skip_group_check=True)
                        if not first or j >= 1:
                            pe.matmul(bk_[:, :, :], ones[:, :], oh[(j - 1) % 4][:, :], start=False, stop=False,
                                      skip_group_check=True)
                        pe.matmul(bk_[:, :, :], before[:, :], oh[j % 4][:, :], start=False, stop=False,
                                  skip_group_check=True).then_inc(S("before"), 1)

            pe.wait_ge(S("blocks"), 3)
            for a, bk_ in ((bsrc, bH0), (bdst, bH1), (bout, bMLP)):
                for b in range(T):
                    mm = pe.transpose(bk_[:, :, :].rearrange("p t f -> p (t f)")[:, b * EB:(b + 1) * EB],
                                      a[:, b, :], ident[0:EB, 0:EB])
                mm.then_inc(S("s_turned"), 1)

            pe.wait_ge(S("ld_const"), 16 * 19)
            for c in range(HC):
                mm = pe.matmul(bT1[:, c, 0:1], W1u[:, c * P:(c + 1) * P], ucol[:, :], start=True, stop=True)
            mm.then_inc(S("u_part"), 1)
            pe.wait_ge(S("b1u"), 1)
            pe.wait_ge(S("s_tabs"), 5)
            pe.wait_ge(S("W_ready"), 2)
            pe.wait_ge(S("ld_bias"), 48)
            pe.wait_ge(S("consts"), 1)

            def turn(dst, tiles):
                for t in range(T):
                    mm = pe.transpose(dst[:, t, :], tiles[t], ident[:, :])
                return mm

            def z_turn(k, i):
                for s in range(2):
                    at(pe, "gathered", s, (seq({3: 5, 4: 6}.get(k, k), i) + 1) * 64)
                    if k == 3:
                        prior(pe, "att_src", s, i)
                    else:
                        prior(pe, "weighted", s, seq(min(k, 3), i))
                    turn(bIN, [gat[s][:, t, 0:P] for t in range(T)]).then_inc(S("turned", s), 1)

            def z_back(k, i):
                for s in range(2):
                    ready(pe, "scanned", s, seq(k if k < 2 else 3, i))
                    if k < 2:
                        prior(pe, "z_rows", s, seq(k, i))
                    else:
                        prior(pe, "fin_sum", s, i)
                    turn(bBK, [zT[s][:, t * P:(t + 1) * P] for t in range(T)]).then_inc(S("back", s), 1)

            def chain_a(kind, i, s):
                c = ci(kind, i)
                prior(pe, "ln1_out", s, c)
                if kind == "s":
                    ready(pe, "x_src", s, i)
                    ready(pe, "ld_z", s, i, 48)
                else:
                    ready(pe, "ld_x", s, i, 16)
                bias(bT1, 0)
                for t in range(T):
                    mm = pe.matmul(bT1[:, t, :], xT[s][:, t, :], W0I[:, 0, :], start=False,
                                   stop=kind == "node", skip_group_check=True)
                    if kind == "s":
                        for k in range(3):
                            mm = pe.matmul(bT1[:, t, :], zin[k][s][:, t, :], W0I[:, k + 1, :], start=False,
                                           stop=k == 2, skip_group_check=True)
                mm.then_inc(S("mm1", s), 1)

            def bias(bank_, k):
                pe.matmul(bank_[:, :, :], ones3[:, :], bias3[:, k:k + 1, :].to_broadcast([3, T, P]),
                          start=True, stop=False, skip_group_check=True)

            def chain_b(kind, i, s):
                c = ci(kind, i)
                if kind == "d":
                    at(pe, "gathered", s, (seq(4, i) + 1) * 64)
                else:
                    ready(pe, "ln1_out", s, c)
                if s == 1:
                    at(pe, "x1T", 0, c + 1)
                elif kind == "d":
                    at(pe, "x2sel", 1, i)
                else:
                    at(pe, "x2T", 1, c)
                rows = gat[s] if kind == "d" else x1[s]
                turn(bTR, [rows[:, t, 0:P] for t in range(T)]).then_inc(S("x1_turned", s), 1)
                ready(pe, "x1T", s, c)
                prior(pe, "relu", s, c)
                if kind == "d":
                    ready(pe, "ld_att", s, i, 32)
                for h in range(HC):
                    cols = slice(h * P, (h + 1) * P)
                    mm = pe.matmul(bH[h][:, :, :], W1x[:, cols], x1T[s][:, :], start=True, stop=kind != "d")
                    if kind == "d":
                        pe.matmul(bH[h][:, :, :], W1a[0:AK, cols], att[s][0:AK, :], start=False, stop=False)
                        mm = pe.matmul(bH[h][:, :, :], W1m[0:AF, cols], mnt[s][:, :], start=False, stop=True)
                mm.then_inc(S("hidden", s), 1)

            def chain_c(kind, i, s):
                c = ci(kind, i)
                ready(pe, "relu", s, c)
                prior(pe, "t2", s, c)
                bias(bMLP, 1)
                for t in range(T):
                    for h in range(HC):
                        mm = pe.matmul(bMLP[:, t, :], hT[h][s][:, t * P:(t + 1) * P], W2s[:, h, :], start=False,
                                       stop=h == HC - 1, skip_group_check=True)
                mm.then_inc(S("mlp", s), 1)

            def chain_d(kind, i, s):
                c = ci(kind, i)
                ready(pe, "ln2_out", s, c)
                if s == 0:
                    at(pe, "x1T", 1, c + 1)
                elif kind == "d":
                    at(pe, "x2sel", 0, i + 1)
                else:
                    at(pe, "x2T", 0, c + 1)
                turn(bTR, [x2[s][:, t, :] for t in range(T)]).then_inc(S("x2_turned", s), 1)
                if kind == "d":
                    return
                ready(pe, "x2T", s, c)
                prior(pe, "ln3_out", s, c)
                skip(x2T[s], bSK, S("skip", s))

            def skip(lhs, dst, sem):
                bias(dst, 2)
                for t in range(T):
                    mm = pe.matmul(dst[:, t, :], lhs[:, t, :], WsI[:, :], start=False, stop=True,
                                   skip_group_check=True)
                mm.then_inc(sem, 1)

            for k in range(2):
                @repeated(pe, EI)
                def _(i):
                    c = i + DPP * k
                    chain_a("node", c, 0)
                    chain_a("node", c, 1)
                    z_turn(k, i)
                    chain_b("node", c, 0)
                    chain_b("node", c, 1)
                    z_back(k, i)
                    chain_c("node", c, 0)
                    chain_c("node", c, 1)
                    chain_d("node", c, 0)
                    chain_d("node", c, 1)

            @repeated(pe, EI)
            def _(i):
                z_turn(2, i)

            for s in range(2):
                at(pe, "weighted", s, 3 * EI)

            @repeated(pe, EI)
            def _(i):
                for s in range(2):
                    at(pe, "gathered", s, (seq(3, i) + 1) * 64)
                    prior(pe, "x_src", s, i)
                    turn(bIN, [gat[s][:, t, 0:P] for t in range(T)]).then_inc(S("turned", s), 1)
                for stage in (chain_a, chain_b, chain_c, chain_d):
                    for s in range(2):
                        stage("s", i, s)

            for s in range(2):
                at(pe, "x2T", s, NI + EI)

            @repeated(pe, EI)
            def _(i):
                for stage in (chain_b, chain_c, chain_d):
                    for s in range(2):
                        stage("d", i, s)

            for s in range(2):
                at(pe, "x_src", s, EI)
                at(pe, "ln1_out", s, NI + EI)
                at(pe, "ln3_out", s, NI + EI)
                at(pe, "t2", s, NI + 2 * EI)
                at(pe, "relu", s, NI + 2 * EI)
                at(pe, "x2sel", s, EI)

            def att_qk(i, s):
                ready(pe, "ld_x2d", s, i, 32)
                prior(pe, "q_out", s, i)
                pe.matmul(bT1[:, :, :], Wqs[:, :], x2d[s][:, :], start=True, stop=True).then_inc(S("q_mm", s), 1)
                ready(pe, "att_src", s, i)
                prior(pe, "qk", s, i)
                pe.matmul(bMLP[:, :, :], Wks[:, :], xs[s][:, :], start=True, stop=True).then_inc(S("k_mm", s), 1)

            def att_v(i, s):
                ready(pe, "att_src", s, i)
                prior(pe, "weighted_v", s, i)
                pe.matmul(bH0[:, :, :], Wvs[:, :], xs[s][:, :], start=True, stop=True).then_inc(S("v_mm", s), 1)

            def att_alpha(i, s):
                ready(pe, "qk", s, i)
                prior(pe, "centred", s, i)
                pe.matmul(bSK[:, :, :], heads[:, :], prod[s][:, :], start=True, stop=True).then_inc(S("alpha", s), 1)

            def att_base(i, s):
                ready(pe, "ld_x2d", s, i, 32)
                prior(pe, "t3", s, i)
                skip(x2d[s][:, :].rearrange("p (t f) -> p t f", t=T), bBK, S("skip_e", s))

            def att_back(i, s):
                ready(pe, "agg", s, i)
                prior(pe, "agg_norm", s, i)
                turn(bTR, [agg[s][:, t * P:(t + 1) * P] for t in range(T)])
                for t in range(T):
                    mm = pe.matmul(bH1[:, 0, 2 * t:2 * t + 2], den[s][:, t * P:(t + 1) * P], hsel[:, :],
                                   start=True, stop=True, skip_group_check=True)
                mm.then_inc(S("agg_turned", s), 1)

            @repeated(pe, EI)
            def _(i):
                z_turn(3, i)
                att_qk(i, 0)
                att_qk(i, 1)
                att_v(i, 0)
                att_alpha(i, 0)
                att_alpha(i, 1)
                att_base(i, 0)
                att_v(i, 1)
                att_back(i, 0)
                att_base(i, 1)
                att_back(i, 1)

            for s in range(2):
                at(pe, "att_src", s, EI)
                at(pe, "t3", s, EI)

            @repeated(pe, EI)
            def _(i):
                z_turn(4, i)
                z_back(2, i)

        @block.scalar
        def _(act):
            act.wait_ge(S("u_part"), 1)
            for c in range(HC):
                a = act.activation(b1u[:, c:c + 1], bT1[:, c, 0:1], ACT.Identity, bias=b1c[:, c:c + 1])
            a.then_inc(S("b1u"), 1)
            act.wait_ge(S("b1u"), 1)
            act.wait_ge(S("consts"), 1)

            def evac(dst, src, sem):
                act.copy(dst, src).then_inc(sem, 1)

            def std(where, k, s, i):
                at(act, "variance", s, norms(where, k, i))
                _, mv, sd, _ = lns[where, k]
                act.activation(sd[s][:, :], mv[s][:, :, 1], ACT.Sqrt, bias=epsc[:, :]).then_inc(S("deviation", s), 1)

            def z_rows(k, i):
                for s in range(2):
                    ready(act, "back", s, seq(k, i))
                    if k == 0:
                        reuse(act, "scattered", s, i, 64)
                    else:
                        reuse(act, "st_z2", s, i, 16)
                    evac(zE[s][:, :, 0:P], bBK[:, :, :], S("z_rows", s))

            def chain_b1(kind, i, s):
                c = ci(kind, i)
                ready(act, "x1_turned", s, c)
                evac(x1T[s][:, :], flat(bTR), S("x1T", s))

            def chain_b2(kind, i, s):
                c = ci(kind, i)
                ready(act, "hidden", s, c)
                reuse(act, "mlp", s, c)
                for h in range(HC):
                    a = act.activation(hT[h][s][:, :], flat(bH[h]), ACT.Relu, bias=b1u[:, h:h + 1])
                a.then_inc(S("relu", s), 1)

            def chain_d(kind, i, s):
                c = ci(kind, i)
                ready(act, "x2_turned", s, c)
                reuse(act, "skip", s, c)
                evac(x2T[s][:, :, :], bTR[:, :, :], S("x2T", s))

            def chain(kind, i, between=lambda: None):
                for s in range(2):
                    if kind != "d":
                        std(kind, 0, s, i)
                for s in range(2):
                    chain_b1(kind, i, s)
                    chain_b2(kind, i, s)
                between()
                for s in range(2):
                    std(kind, 1, s, i)
                if kind == "d":
                    return
                for s in range(2):
                    chain_d(kind, i, s)
                for s in range(2):
                    std(kind, 2, s, i)
                if kind == "node":
                    for s in range(2):
                        std(kind, 3, s, i)

            for k in range(2):
                @repeated(act, EI)
                def _(i):
                    chain("node", i + DPP * k, lambda: z_rows(k, i))
            for s in range(2):
                at(act, "st_z2", s, EI * 16)

            @repeated(act, EI)
            def _(i):
                for s in range(2):
                    ready(act, "turned", s, seq(3, i))
                    reuse(act, "mm1", s, ci("s", i))
                    evac(xT[s][:, :, :], bIN[:, :, :], S("x_src", s))
                chain("s", i)

            @repeated(act, EI)
            def _(i):
                chain("d", i)

            @repeated(act, EI)
            def _(i):
                for s in range(2):
                    ready(act, "turned", s, seq(4, i))
                    reuse(act, "v_mm", s, i)
                    evac(xs[s][:, :], flat(bIN), S("att_src", s))
                for s in range(2):
                    ready(act, "q_mm", s, i)
                    reuse(act, "qk", s, i)
                    act.activation(qT[s][:, :], flat(bT1), ACT.Identity, bias=bqc[:, :]).then_inc(S("q_out", s), 1)
                for s in range(2):
                    ready(act, "delta", s, i)
                    reuse(act, "agg", s, i)
                    act.activation(dec[s], dlt[s], ACT.Exp).then_inc(S("decay", s), 1)
                    ready(act, "centred", s, i)
                    act.activation(aw[s][:, :], elt[s], ACT.Exp).then_inc(S("weight", s), 1)
                for s in range(2):
                    std("att", 2, s, i)
                for s in range(2):
                    std("att", 3, s, i)

            @repeated(act, EI)
            def _(i):
                for s in range(2):
                    std("fin", 3, s, i)

        @block.vector
        def _(dve):
            dve.memset(W1a[:, :], 0.0)
            dve.memset(W1m[:, :], 0.0).then_inc(S("init_w1"), 1)
            dve.memset(zeros[:, :], 0.0).then_inc(S("init_zero"), 1)
            dve.memset(ones3[:, :], 1.0)
            dve.memset(epsc[:, :], EPS)
            dve.memset(heads[:, :], 0.0)
            dve.memset(hsel[:, :], 0.0).then_inc(S("heads0"), 1)
            dve.memset(onesE[:, :], 1.0)
            dve.wait_ge(S("heads0"), 1)
            C = P // 2
            for h in range(2):
                dve.memset(heads[h * C:(h + 1) * C, h * C:(h + 1) * C], float(C) ** -0.5)
                dve.memset(hsel[h * C:h * C + 1, h:h + 1], 1.0)
            dve.memset(ctmp[:, :], 0.0).then_inc(S("consts"), 1)
            dve.wait_ge(S("ld_flat"), 48)
            dve.tensor_copy(payl[:, :, 0], fsrc[:, :]).then_inc(S("payload"), 1)
            dve.tensor_copy(payl[:, :, 1], fdst[:, :]).then_inc(S("payload"), 1)
            dve.memset(payl[:, :, 3], 0)
            dve.tensor_copy(payl[:, :, 2].bitcast(F32), fw[:, :]).then_inc(S("payload"), 1)
            dve.wait_ge(S("ld_gsrc"), 16)
            dve.wait_ge(S("enum_i"), 2)

            def digit(k, dst, src):
                if k == 0:
                    return dve.tensor_scalar(dst, src, NB - 1, None, ALU.bitwise_and)
                return dve.tensor_scalar(dst, src, DIG, None, ALU.arith_shift_right)

            digit(0, digi[:, 0, :], gsrc[:, :])
            digit(1, digi[:, 1, :], gsrc[:, :])
            dve.tensor_copy(buckets[:, :], buckets_i[:, :])
            dve.drain()
            dve.tensor_copy(digf[:, :, :], digi[:, :, :])
            dve.drain()

            dve.wait_ge(S("ld_prep"), 80)
            dve.tensor_tensor(same[:, :], dstc[:, :], dstp[:, :], ALU.is_equal).then_inc(S("prep"), 1)
            dve.tensor_tensor(notlast[:, :], dstc[:, :], dstn[:, :], ALU.is_equal)
            dve.tensor_tensor(last[:, :], dstc[:, :], dstn[:, :], ALU.not_equal)
            dve.tensor_tensor(geq[:, :], gdst[:, :], gdn[:, :], ALU.is_equal)
            dve.drain()
            dve.tensor_scalar(samem[:, :], same[:, :], 0.5, FMAX, ALU.subtract, ALU.mult).then_inc(S("prep"), 1)
            dve.wait_ge(S("prep"), 2)
            dve.tensor_scalar(samem[:, :], samem[:, :], 2.0, None, ALU.mult).then_inc(S("flags"), 1)
            dve.tensor_scalar(ctmp[:, :], geq[:, :], float(BIG), None, ALU.mult)
            dve.tensor_scalar(ctmp2[:, :], gdst[:, :], 3.0, None, ALU.mult)
            dve.drain()
            dve.tensor_tensor(tabs["d_out"][:, :], ctmp[:, :], gdst[:, :], ALU.add).then_inc(S("d_tabs"), 1)
            dve.tensor_copy(tabs["d_x1"][:, :], ctmp2[:, :]).then_inc(S("d_tabs"), 1)
            dve.tensor_scalar(tabs["d_x2s"][:, :], gsrc[:, :], 3.0, 1.0, ALU.mult, ALU.add).then_inc(S("d_tabs"), 1)
            dve.tensor_tensor(ctmp[:, :], ctmp[:, :], ctmp2[:, :], ALU.add).then_inc(S("d_tabs"), 1)
            dve.drain()
            dve.tensor_scalar(tabs["d_x2_out"][:, :], ctmp[:, :], 1.0, None, ALU.add).then_inc(S("d_tabs"), 1)
            dve.tensor_scalar(tabs["d_x3_out"][:, :], ctmp[:, :], 2.0, None, ALU.add).then_inc(S("d_tabs"), 1)
            dve.tensor_copy(enum[:, :], enum_i[:, :]).then_inc(S("enum"), 1)
            dve.tensor_tensor_scan(cntl[:, :], same[:, :], onesE[:, :], 0.0, ALU.mult, ALU.add
                                   ).then_inc(S("cnt_local"), 1)
            dve.drain()
            dve.memset(ctmp[:, :], 0.0)
            dve.drain()
            dve.tensor_tensor_scan(allsame[:, :], same[:, :], ctmp[:, :], 1.0, ALU.mult, ALU.add
                                   ).then_inc(S("cnt_local"), 1)
            dve.wait_ge(S("carry_row"), 16)
            dve.tensor_tensor_scan(crow[:, 2, :], crow[:, 1, :], crow[:, 0, :], 0.0, ALU.mult, ALU.add
                                   ).then_inc(S("carry_scan"), 1)
            dve.wait_ge(S("carry_col"), 16)
            dve.scalar_tensor_tensor(out=ctmp[:, :], in0=allsame[:, :], scalar=ccol[:, 0:1], in1=cntl[:, :],
                                     op0=ALU.mult, op1=ALU.add).then_inc(S("prep"), 1)
            dve.wait_ge(S("prep"), 3)
            dve.reciprocal(inv[:, :], ctmp[:, :]).then_inc(S("inv"), 1)
            dve.wait_ge(S("ld_const"), 16 * 19)
            dve.wait_ge(S("ident"), 1)
            dve.tensor_tensor(W0I[:, 0, :], W0I[:, 0, :], ident[:, :], ALU.add).then_inc(S("W_ready"), 1)
            dve.tensor_tensor(WsI[:, :], WsI[:, :], ident[:, :], ALU.add).then_inc(S("W_ready"), 1)
            left = brow
            for k in range(3):
                dve.tensor_copy(bsp[:, k, :, :], left[:, :, :]).then_inc(S("bias_split"), 1)
                if k < 2:
                    dve.wait_ge(S("bias_split"), k + 1)
                    nxt = [bres, bres2][k]
                    dve.tensor_tensor(nxt[:, :, :], left[:, :, :], bsp[:, k, :, :], ALU.subtract
                                      ).then_inc(S("prep"), 1)
                    dve.wait_ge(S("prep"), k + 4)
                    left = nxt
            @repeated(dve, EI)
            def _(i):
                for j in range(TI):
                    c = i * TI + j
                    tiles_done(dve, "counted", tile_no(0, i, j - 3))
                    for o, k in ((oh, 0), (ohh, 1)):
                        a = dve.tensor_scalar(o[j % 4][:, :], buckets[:, :], digf[:, k, bass.ds(c, 1)], None,
                                              ALU.is_equal)
                    a.then_inc(S("one_hot"), 1)
            dve.wait_ge(S("counted"), EC)
            for k, bk_ in enumerate((bT1, bTR)):
                dve.tensor_tensor_scan(hscan[:, k, :], flat(bk_), hzero[:, :], 0.0,
                                       ALU.add, ALU.add)
            dve.drain()
            for k, bk_ in enumerate((bT1, bTR)):
                dve.tensor_tensor(base[:, k, :], hscan[:, k, :], flat(bk_), ALU.subtract).then_inc(S("bases"), 1)

            for k in (1, 2):
                pair = (bH0, bH1) if k == 1 else (bMLP, bSK)

                @repeated(dve, EI)
                def _(i):
                    def one_hot(j):
                        tiles_done(dve, "before", tile_no(k - 1, i, j - 1))
                        dve.tensor_scalar(oh[j % 4][:, :], buckets[:, :], dig4[j // T][:, j % T:j % T + 1], None,
                                          ALU.is_equal).then_inc(S("one_hot"), 1)

                    for s in range(2):
                        at(dve, "ld_pay", s, (i + ((k - 1) * EI + 1)) * 16)
                        digit(k - 1, dig4i[s][:, :], pay[s][:, :, 0])
                    dve.drain()
                    for s in range(2):
                        dve.tensor_copy(dig4[s][:, :], dig4i[s][:, :])
                    dve.drain()
                    one_hot(0)
                    for j in range(TI):
                        s = j // T
                        if j + 1 < TI:
                            one_hot(j + 1)
                        tiles_done(dve, "before", tile_no(k - 1, i, j + 1))
                        dve.scalar_tensor_tensor(out=junk[j % 2][:, :], in0=flat(pair[j % 2]), scalar=1.0, in1=oh[j % 4][:, :],
                                                 op0=ALU.mult, op1=ALU.mult,
                                                 accum_out=pos4[s][:, j % T:j % T + 1]).then_inc(S("ranked_tile"), 1)
                        if j % T == T - 1:
                            dve.wait_ge(S("ranked_tile"), tile_no(k - 1, i, j + 1))
                            at(dve, "placed", s, (i + (k - 1) * EI) * 64)
                            dve.tensor_scalar(idx[s][:, :], pos4[s][:, :], 1.0, None, ALU.add
                                              ).then_inc(S("ranked", s), 1)

            dve.wait_ge(S("ld_blocks"), 48)
            dve.tensor_tensor(bsame[:, :, :], pb[1][:, :, :, 0], pb[0][:, :, :, 0], ALU.is_equal
                              ).then_inc(S("s_rows"), 1)
            dve.tensor_copy(bw[:, :, :], pb[1][:, :, :, 2].bitcast(F32)).then_inc(S("s_rows"), 1)
            dve.tensor_copy(bsrc[:, :, :], pb[1][:, :, :, 0]).then_inc(S("blocks"), 1)
            dve.tensor_copy(bdst[:, :, :], pb[1][:, :, :, 1]).then_inc(S("blocks"), 1)
            dve.tensor_tensor(bout[:, :, :], pb[1][:, :, :, 0], pb[2][:, :, :, 0], ALU.is_equal)
            dve.drain()
            dve.scalar_tensor_tensor(out=bout[:, :, :], in0=bout[:, :, :], scalar=float(BIG), in1=pb[1][:, :, :, 0],
                                     op0=ALU.mult, op1=ALU.add).then_inc(S("blocks"), 1)
            dve.wait_ge(S("s_turned"), 3)
            tsrc, tdst, tout = (flat(b)[:, 0:EC] for b in (bH0, bH1, bMLP))
            dve.tensor_copy(tabs["s_dst"][:, :], tdst).then_inc(S("s_tabs"), 1)
            dve.tensor_copy(tabs["s_src"][:, :], tsrc).then_inc(S("s_tabs"), 1)
            dve.tensor_copy(tabs["s_out"][:, :], tout).then_inc(S("s_tabs"), 1)
            dve.tensor_scalar(tabs["s_x3d"][:, :], tdst, 3.0, 2.0, ALU.mult, ALU.add).then_inc(S("s_tabs"), 1)
            dve.tensor_scalar(tabs["s_x3s"][:, :], tsrc, 3.0, 2.0, ALU.mult, ALU.add).then_inc(S("s_tabs"), 1)

            prepared(dve)
            for s in range(2):
                dve.memset(att[s][:, :], 0.0)
                dve.memset(zT[s][:, :], 0.0)
                dve.memset(zE[s][:, :, :], 0.0)
                dve.memset(mbuf[s][:, :], 0.0)
                dve.memset(x2d[s][:, :], 0.0).then_inc(S("carry0"), 1)
            dve.wait_ge(S("carry0"), 2)
            dve.wait_ge(S("enum"), 1)

            def stats(where, k, src, s, i):
                st, mv, _, _ = lns[where, k]
                for t in range(T):
                    a = dve.bn_stats(st[s][:, t, :], src[:, t, :])
                dve.drain()
                for t in range(T):
                    a = dve.bn_aggr(mv[s][:, t, :], st[s][:, t, :])
                a.then_inc(S("variance", s), 1)

            def norm(where, k, src, dst, s, i, done):
                _, mv, sd, rs = lns[where, k]
                at(dve, "deviation", s, norms(where, k, i))
                dve.reciprocal(rs[s][:, :], sd[s][:, :]).then_inc(S("scale", s), 1)
                at(dve, "scale", s, norms(where, k, i))
                for t in range(T):
                    a = dve.tensor_scalar(dst[:, t, :], src[:, t, :], mv[s][:, t, 0:1], rs[s][:, t:t + 1],
                                          ALU.subtract, ALU.mult)
                a.then_inc(S(done, s), 1)

            def z_scan(k, i):
                for s in range(2):
                    c = seq(k, i)
                    ready(dve, "turned", s, seq(5 if k == 3 else k, i))
                    ready(dve, "ld_row", s, c, 32)
                    dve.tensor_tensor(msg[s][:, :], flat(bIN), wB[s][:, :], ALU.mult).then_inc(S("weighted", s), 1)
                    if k == 1:
                        dve.tensor_copy(codes[:, bass.ds((i * 2 + s) * T, T)], gat[s][:, :, P]
                                        ).then_inc(S("coded", s), 1)
                    if k < 3:
                        reuse(dve, "st_zT", s, c, 16)
                    if k != 2:
                        at(dve, "back", s, i + (k if k < 2 else 2) * EI)
                    ready(dve, "weighted", s, c)
                    prior(dve, "scanned", s, c)
                    dve.tensor_tensor_scan(zT[s][:, :], fB[s][:, :], msg[s][:, :], zT[1 - s][:, G - 1:G],
                                           ALU.mult, ALU.add).then_inc(S("scanned", s), 1)
                    if k == 0:
                        reuse(dve, "scattered", s, i, 64)
                        dve.tensor_copy(zE[s][:, :, P], enum[:, bass.ds((i * 2 + s) * T, T)]
                                        ).then_inc(S("numbered", s), 1)

            def chain_1(kind, i):
                for s in range(2):
                    c = ci(kind, i)
                    ready(dve, "mm1", s, c)
                    stats(kind, 0, bT1, s, i)
                    reuse(dve, "x1_turned", s, c)
                    if kind == "node":
                        reuse(dve, "st_xt", s, i, 16)
                    else:
                        at(dve, "scattered", s, seq(1, i) * 64)
                    norm(kind, 0, bT1, x1[s], s, i, "ln1_out")

            def chain_2(kind, i):
                for s in range(2):
                    c = ci(kind, i)
                    ready(dve, "mlp", s, c)
                    rows = gat[s][:, :, 0:P] if kind == "d" else x1[s]
                    dve.scalar_tensor_tensor(out=t2[s][:, :, :], in0=rows, scalar=2.0, in1=bMLP[:, :, :],
                                             op0=ALU.mult, op1=ALU.add).then_inc(S("t2", s), 1)
                    ready(dve, "t2", s, c)
                    stats(kind, 1, t2[s], s, i)
                for s in range(2):
                    if kind == "d":
                        at(dve, "scattered", s, seq(2, i) * 64)
                    norm(kind, 1, t2[s], x2[s], s, i, "ln2_out")

            def chain_3(kind, i):
                for s in range(2):
                    ready(dve, "skip", s, ci(kind, i))
                    stats(kind, 2, bSK, s, i)
                    norm(kind, 2, bSK, x3[s], s, i, "ln3_out")

            def layer4_alone(kind, i, c3, c4):
                for s in range(2):
                    ready(dve, "ln3_out", s, c3)
                    dve.tensor_scalar(t2[s][:, :, :], x3[s], 1.25, None, ALU.mult)
                    dve.drain()
                    stats(kind, 3, t2[s], s, i)
                for s in range(2):
                    if kind == "node":
                        reuse(dve, "st_x4", s, i, 16)
                    else:
                        reuse(dve, "scattered2", s, i, 64)
                    norm(kind, 3, t2[s], x4[s], s, i, "ln4_out")

            for k in range(2):
                @repeated(dve, EI)
                def _(i):
                    c = i + DPP * k
                    chain_1("node", c)
                    z_scan(k, i)
                    chain_2("node", c)
                    chain_3("node", c)
                    layer4_alone("node", c, c, c)

            for s in range(2):
                at(dve, "coded", s, EI)
                at(dve, "st_xt", s, NI * 16)
                at(dve, "st_x4", s, NI * 16)
            dve.tensor_copy(tabs["s_z"][:, :], codes[:, :]).then_inc(S("s_ztab"), 1)

            def attr_scan(i, s):
                ready(dve, "ld_attr", s, i, 80)
                reuse(dve, "st_att", s, i, 32)
                prior(dve, "attr_sums", s, i)
                dve.tensor_tensor_scan(att[s][0:AF, :], f2B[s][0:AF, :], atr[s][0:AF, :],
                                       att[1 - s][0:AF, G - 1:G], ALU.mult, ALU.add)
                dve.tensor_tensor_scan(att[s][AM:AK, :], fmB[s][AM:AK, :], atr[s][AM:AK, :],
                                       att[1 - s][AM:AK, G - 1:G], ALU.min, ALU.max).then_inc(S("attr_sums", s), 1)
                ready(dve, "attr_sums", s, i)
                dve.tensor_tensor(mnt[s][:, :], att[s][0:AF, :], invB[s][0:AF, :], ALU.mult
                                  ).then_inc(S("attr_mean", s), 1)

            @repeated(dve, EI)
            def _(i):
                for s in range(2):
                    attr_scan(i, s)
                z_scan(2, i)

            @repeated(dve, EI)
            def _(i):
                chain_1("s", i)
                chain_2("s", i)
                chain_3("s", i)
            for s in range(2):
                at(dve, "scattered", s, 2 * EI * 64)

            @repeated(dve, EI)
            def _(i):
                chain_2("d", i)
                for s in range(2):
                    ready(dve, "x2_turned", s, ci("d", i))
                    ready(dve, "ld_last", s, i, 32)
                    dve.tensor_tensor(msg[s][:, :], flat(bTR), f2B[s][:, :], ALU.mult).then_inc(S("x2sel", s), 1)
                    reuse(dve, "st_x2d", s, i, 16)
                    ready(dve, "x2sel", s, i)
                    prior(dve, "x2d", s, i)
                    dve.tensor_tensor_scan(x2d[s][:, ::-1], fmB[s][:, ::-1], msg[s][:, ::-1], x2d[1 - s][:, 0:1],
                                           ALU.mult, ALU.add).then_inc(S("x2d", s), 1)

            def att_scores(i, s):
                ready(dve, "k_mm", s, i)
                ready(dve, "q_out", s, i)
                reuse(dve, "alpha", s, i)
                dve.scalar_tensor_tensor(out=prod[s][:, :], in0=bMLP[:, :, :].rearrange("p t f -> p (t f)"),
                                         scalar=bkc[:, 0:1], in1=qT[s][:, :], op0=ALU.add, op1=ALU.mult
                                         ).then_inc(S("qk", s), 1)

            def att_max(i, s):
                alpha = bSK[:, :, :].rearrange("p t f -> p (t f)")
                ready(dve, "alpha", s, i)
                ready(dve, "ld_x2d", s, i, 32)
                prior(dve, "maxed", s, i)
                reuse(dve, "decayed", s, i)
                dve.tensor_tensor_scan(mbuf[s][:, 1:G + 1], fmB[s][:, :], alpha, mbuf[1 - s][:, G:G + 1],
                                       ALU.min, ALU.max)
                dve.tensor_copy(mbuf[s][:, 0:1], mbuf[1 - s][:, G:G + 1]).then_inc(S("maxed", s), 1)
                ready(dve, "maxed", s, i)
                reuse(dve, "decay", s, i)
                dve.tensor_tensor(dlt[s], fmB[s][:, :], mbuf[s][:, 0:G], ALU.min).then_inc(S("decayed", s), 1)
                reuse(dve, "weight", s, i)
                dve.tensor_tensor(elt[s], alpha, mbuf[s][:, 1:G + 1], ALU.subtract).then_inc(S("centred", s), 1)
                ready(dve, "decayed", s, i)
                dve.tensor_tensor(dlt[s], dlt[s], mbuf[s][:, 1:G + 1], ALU.subtract).then_inc(S("delta", s), 1)

            def att_sum(i, s):
                ready(dve, "weight", s, i)
                ready(dve, "v_mm", s, i)
                dve.scalar_tensor_tensor(out=av[s][:, :], in0=bH0[:, :, :].rearrange("p t f -> p (t f)"),
                                         scalar=bvc[:, 0:1], in1=aw[s][:, :], op0=ALU.add, op1=ALU.mult
                                         ).then_inc(S("weighted_v", s), 1)
                ready(dve, "decay", s, i)
                reuse(dve, "agg_turned", s, i)
                prior(dve, "agg", s, i)
                dve.tensor_tensor_scan(den[s][:, :], dec[s], aw[s][:, :], den[1 - s][:, G - 1:G], ALU.mult, ALU.add)
                ready(dve, "weighted_v", s, i)
                dve.tensor_tensor_scan(agg[s][:, :], dec[s], av[s][:, :], agg[1 - s][:, G - 1:G], ALU.mult, ALU.add
                                       ).then_inc(S("agg", s), 1)

            def att_out(i, s):
                ready(dve, "agg_turned", s, i)
                dve.tensor_scalar(dmax[s][:, :], bH1[:, 0, 0:2 * T], 1e-16, None, ALU.max).then_inc(S("dmax", s), 1)
                ready(dve, "dmax", s, i)
                dve.reciprocal(rden[s][:, :], dmax[s][:, :]).then_inc(S("rden", s), 1)
                ready(dve, "rden", s, i)
                C = P // 2
                dve.tensor_tensor(flat(aggn[s]).rearrange("p (h c) -> p h c", c=C),
                                  bTR[:, :, :].rearrange("p t f -> p (t f)").rearrange("p (h c) -> p h c", c=C),
                                  rden[s][:, :].rearrange("p (h a) -> p h a", a=1).to_broadcast([P, 2 * T, C]),
                                  ALU.mult).then_inc(S("agg_norm", s), 1)
                ready(dve, "agg_norm", s, i)
                ready(dve, "skip_e", s, i)
                dve.tensor_tensor(t2[s][:, :, :], bBK[:, :, :], aggn[s][:, :, :], ALU.add).then_inc(S("t3", s), 1)
                ready(dve, "t3", s, i)
                stats("att", 2, t2[s], s, i)

            for s in range(2):
                at(dve, "x2d", s, EI)
                at(dve, "scattered", s, 3 * EI * 64)
                at(dve, "hidden", s, NI + 2 * EI)
                dve.memset(den[s][:, :], 0.0)
                dve.memset(agg[s][:, :], 0.0).then_inc(S("sums0"), 1)
            dve.wait_ge(S("sums0"), 2)

            @repeated(dve, EI)
            def _(i):
                for stage in (att_scores, att_max, att_sum, att_out):
                    for s in range(2):
                        stage(i, s)
                for s in range(2):
                    at(dve, "scattered", s, seq(3, i) * 64)
                    norm("att", 2, t2[s], x3[s], s, i, "ln3_out")
                layer4_alone("att", i, i + NI + EI, i + NI)

            for s in range(2):
                at(dve, "agg", s, EI)
                at(dve, "scattered2", s, EI * 64)
            dve.memset(zT[1][:, :], 0.0).then_inc(S("sums0"), 1)
            dve.wait_ge(S("sums0"), 3)

            @repeated(dve, EI)
            def _(i):
                z_scan(3, i)
                for s in range(2):
                    ready(dve, "gathered2", s, i, 64)
                    dve.tensor_scalar(x2T[s][:, :, :], own[s][:, :, :], 1.25, None, ALU.mult
                                      ).then_inc(S("fin_scaled", s), 1)
                    ready(dve, "back", s, seq(2, i))
                    ready(dve, "fin_scaled", s, i)
                    dve.scalar_tensor_tensor(out=t2[s][:, :, :], in0=bBK[:, :, :], scalar=0.75, in1=x2T[s][:, :, :],
                                             op0=ALU.mult, op1=ALU.add).then_inc(S("fin_sum", s), 1)
                    ready(dve, "fin_sum", s, i)
                    stats("fin", 3, t2[s], s, i)
                for s in range(2):
                    at(dve, "scattered", s, seq(4, i) * 64)
                    norm("fin", 3, t2[s], x4[s], s, i, "ln4_out")


def kernel(**inputs):
    import numpy as np
    import concourse.bacc as bacc
    from concourse.bass_utils import run_bass_kernel_spmd as run

    a = {k: np.asarray(v) for k, v in inputs.items()}
    N, D = a["x"].shape
    E = a["src"].shape[0]
    N_PAD = -(-(N + 1) // (4 * G)) * 4 * G
    E_PAD = -(-E // (2 * G)) * 2 * G
    if N_PAD != 2 * E_PAD:
        N_PAD = max(N_PAD, 2 * E_PAD)
        E_PAD = N_PAD // 2

    def padded(v, n, fill):
        out = np.full((n,) + v.shape[1:], fill, v.dtype)
        out[:v.shape[0]] = v
        return out

    src = padded(a["src"], E_PAD, N_PAD - 1)
    dst = padded(a["dst"], E_PAD, N_PAD - 1)
    dst_flat = np.full((E_PAD + 2,), -1, dst.dtype)
    dst_flat[1:-1] = dst
    x_rows = padded(a["x"], N_PAD, 0)
    arrays = {
        "x_fm": np.ascontiguousarray(x_rows.reshape(-1, P, T, D).transpose(3, 0, 2, 1).reshape(D, N_PAD)),
        "x_rows": x_rows,
        "src_g": np.ascontiguousarray(src.reshape(-1, T, P).transpose(0, 2, 1)),
        "dst_g": np.ascontiguousarray(dst.reshape(-1, T, P).transpose(0, 2, 1)),
        "dnext_g": np.ascontiguousarray(dst_flat[2:].reshape(-1, T, P).transpose(0, 2, 1)),
        "src_flat": src,
        "dst_flat": dst_flat,
        "w_flat": padded(a["edge_weight"], E_PAD, 0),
        "attr_fm": np.ascontiguousarray(padded(a["edge_attr_48"], E_PAD, 0).T),
    }
    for n in ("L0_gnn_W", "L0_gnn_b", "L1_gnn_u", "L1_gnn_W1", "L1_gnn_b1", "L1_gnn_W2", "L1_gnn_b2",
              "L2_gnn_Wq", "L2_gnn_bq", "L2_gnn_Wk", "L2_gnn_bk", "L2_gnn_Wv", "L2_gnn_bv", "L2_gnn_Wskip",
              "L2_gnn_bskip"):
        arrays[n] = np.ascontiguousarray(a[n])
    nc = bacc.Bacc("TRN2", target_bir_lowering=False, num_devices=1)
    args = [nc.dram_tensor("in_" + n, v.shape, mybir.dt.from_np(v.dtype), kind="ExternalInput").ap()
            for n, v in arrays.items()]
    out = nc.dram_tensor("out_rows", (N_PAD, D), F32, kind="ExternalOutput").ap()
    gnn_kernel(nc, *args, out)
    r = run(nc, [{"in_" + n: v for n, v in arrays.items()}], core_ids=[0])
    return r.results[0]["out_rows"][:N]
```

```python
from contextlib import ExitStack

import concourse.bass as bass
from concourse import mybir

F32 = mybir.dt.float32
BF16 = mybir.dt.bfloat16
I32 = mybir.dt.int32
I16 = mybir.dt.int16
ALU = mybir.AluOpType
ACT = mybir.ActivationFunctionType

P = 128
T = 4
G = T * P
SL = 4
EPS = 1e-5
FMAX = 3.4028234e38
BIG = 1 << 23
AM = 64
ZW = P + 4
DIG = 9
NB = 1 << DIG
HB = 32
HA = NB // HB


def gnn_kernel(nc, x_fm, x_rows, src_g, dst_g, dnext_g, src_flat, dst_flat, w_flat, attr_fm,
               W0, b0, u, W1, b1, W2, b2, Wq, bq, Wk, bk, Wv, bv, Ws, bs, out):
    N_PAD, E_PAD = x_rows.shape[0], w_flat.shape[0]
    NI = N_PAD // (SL * G)
    EI = E_PAD // (SL * G)
    EC = E_PAD // P
    EB = EC // T
    AF = attr_fm.shape[0] - AM
    AK = AM + AF
    HID = W1.shape[1]
    HC = HID // P
    UF = u.shape[1]
    DPP = NI // 2
    TI = SL * T
    assert NI == 2 * EI and DPP == EI and EB <= P and N_PAD <= NB * NB and AF <= AM

    ctx = ExitStack()
    with ctx:
        def sb(name, shape, dt=F32):
            return ctx.enter_context(nc.sbuf_tensor(name, shape, dt))

        def dram(name, shape, dt=F32):
            return nc.dram_tensor(name, shape, dt, kind="Internal").ap()

        AFTER = {
            "ld_x": ("ld_pay", 2 * EI * 16), "ld_z": ("ld_x", NI * 16), "ld_x2d": ("ld_z", EI * 48),
            "ld_last": ("ld_attr", EI * 64), "ld_idx2": ("ld_att", EI * 32),
            "st_x2d": ("st_zT", EI * 48), "st_att": ("st_z2", EI * 16),
            "scattered2": ("placed", 2 * EI * 64), "gathered2": ("scattered2", EI * 64),
            "qk": ("coded", EI), "maxed": ("numbered", EI), "decayed": ("x2d", EI), "centred": ("attr_sums", EI),
            "delta": ("attr_mean", EI), "t3": ("x2sel", EI), "fin_scaled": ("weighted_v", EI), "fin_sum": ("agg", EI),
            "q_mm": ("skip", NI + EI), "k_mm": ("x2_turned", NI + 2 * EI), "v_mm": ("hidden", NI + 2 * EI),
            "alpha": ("mlp", NI + 2 * EI), "skip_e": ("x1_turned", NI + 2 * EI), "agg_turned": ("mm1", NI + EI),
            "q_out": ("x1T", NI + 2 * EI), "decay": ("relu", NI + 2 * EI), "weight": ("x2T", NI + EI),
            "att_src": ("z_rows", 2 * EI),
        }

        def first_of(name):
            start = 0
            while name in AFTER:
                name, n = AFTER[name]
                start += n
            return name, start

        BASE = {n: first_of(n)[1] for n in AFTER}
        sems = {}

        def by_slot(name):
            return name.startswith(("ld_", "st_", "gathered", "scattered", "placed"))

        def S(name, s=""):
            key = f"{first_of(name)[0]}{s if by_slot(name) else ''}"
            if key not in sems:
                sems[key] = ctx.enter_context(nc.semaphore(key))
            return sems[key]

        Z1N = dram("Z1N", [N_PAD, ZW])
        Z2E = dram("Z2E", [E_PAD + 1, P])
        XT = dram("XT", [N_PAD, 3 * P])
        XT3 = XT.rearrange("n (k f) -> (n k) f", k=3)
        ZT = [dram(f"Z{k}T", [P, E_PAD]) for k in (1, 2, 3)]
        ATT = dram("ATT", [AK, E_PAD])
        MNT = dram("MNT", [AF, E_PAD])
        X2DT = dram("X2DT", [P, E_PAD])
        PAIRS = {p: dram("rows_" + "_".join(p), [2, E_PAD]) for p in (
            ("same", "samem"), ("last", "notlast"), ("s_same", "s_w"))}
        ROWS = {n: t[k:k + 1, :] for p, t in PAIRS.items() for k, n in enumerate(p)}
        ROWS["inv"] = dram("row_inv", [1, E_PAD])
        TAB = {n: dram(f"tab_{n}", [P, EC], I32) for n in (
            "d_x1", "d_x2_out", "d_x3_out", "d_out",
            "d_x2s",
            "s_dst", "s_src", "s_out",
            "s_x3d", "s_x3s", "s_z")}
        PAY = dram("PAY", [E_PAD + 2, 4], I32)
        PLOW = dram("PLOW", [E_PAD + 2, 4], I32)
        PSRC = dram("PSRC", [E_PAD + 2, 4], I32)
        HIST = dram("HIST", [2, NB])
        cols_d = dram("cols_d", [3, P])

        bank = [ctx.enter_context(nc.psum_tensor(f"bank{b}", [P, T, P], F32)) for b in range(8)]
        bT1, bTR, bH0, bH1, bMLP, bSK, bIN, bBK = bank
        bH = [bH0, bH1]

        ident = sb("ident", [P, P])
        W0I = sb("W0I", [P, 4, P])
        W1x = sb("W1x", [P, HID])
        W1a = sb("W1a", [P, HID])
        W1m = sb("W1m", [P, HID])
        W1u = sb("W1u", [UF, HID])
        ucol = sb("ucol", [UF, 1])
        b1c = sb("b1c", [P, HC])
        b1u = sb("b1u", [P, HC])
        W2s = sb("W2s", [P, HC, P])
        Wqs, Wks, Wvs = sb("Wqs", [P, P]), sb("Wks", [P, P]), sb("Wvs", [P, P])
        bqc, bkc, bvc = sb("bqc", [P, 1]), sb("bkc", [P, 1]), sb("bvc", [P, 1])
        WsI = sb("WsI", [P, P])
        heads = sb("heads", [P, P])
        hsel = sb("hsel", [P, 2])
        epsc = sb("epsc", [P, 1])
        ones3 = sb("ones3", [3, P], BF16)
        brow = sb("brow", [1, 3, P])
        bres = sb("bres", [1, 3, P])
        bres2 = sb("bres2", [1, 3, P])
        bsp = sb("bsp", [1, 3, 3, P], BF16)
        bias3 = sb("bias3", [3, 3, P], BF16)

        tabs = {"s_z": sb("t_s_z", [P, EC], I32)}
        enum = sb("enum", [P, EC])
        codes = sb("codes", [P, EC])
        idx, idx2, sct = ([sb(f"{n}{s}", [P, T], I32) for s in range(SL)] for n in ("idx", "idx2_", "sct"))

        prep_ctx = ExitStack()

        def early(name, shape, dt=F32):
            return prep_ctx.enter_context(nc.sbuf_tensor(name, shape, dt))

        dstp, dstc, dstn = early("dstp", [P, EC], I32), early("dstc", [P, EC], I32), early("dstn", [P, EC], I32)
        same, samem = early("same", [P, EC]), early("samem", [P, EC])
        notlast, last = early("notlast", [P, EC]), early("last", [P, EC])
        onesE = early("onesE", [P, EC])
        cntl, allsame, inv = early("cntl", [P, EC]), early("allsame", [P, EC]), early("inv", [P, EC])
        crow = early("crow", [1, 3, P])
        ccol = early("ccol", [P, 1])
        gdst, gdn = early("gdst", [P, EC], I32), early("gdn", [P, EC], I32)
        gsrc, geq = early("gsrc", [P, EC], I32), early("geq", [P, EC])
        tabs.update((n, early(f"t_{n}", [P, EC], I32)) for n in TAB if n != "s_z")
        enum_i = early("enum_i", [P, EC], I32)
        ctmp, ctmp2 = early("ctmp", [P, EC]), early("ctmp2", [P, EC])
        zeros = early("zeros", [P, 2 * T * ZW])
        hzero = zeros[:, 0:NB]
        fsrc, fdst, fw = early("fsrc", [P, EC], I32), early("fdst", [P, EC], I32), early("fw", [P, EC])
        payl = early("payl", [P, EC, 4], I32)
        parts_i = early("parts_i", [P, 2, 2, EC], I32)
        parts_a, parts_b = early("parts_a", [P, EC, 2]), early("parts_b", [P, EC, 2])
        oha = [early(f"oha{s}", [P, T, 2, HA], BF16) for s in range(SL)]
        ohb = [early(f"ohb{s}", [P, T, 2, HB], BF16) for s in range(SL)]
        hist_s, hist = early("hist_s", [2 * HA, 2 * HB]), early("hist", [P, 2, NB])
        buckets_i, buckets = early("buckets_i", [P, NB], I32), early("buckets", [P, NB], I16)
        oh = [early(f"oh{r}", [P, NB], BF16) for r in range(4)]
        before, rest, ones = early("before", [P, P], BF16), early("rest", [P, P], BF16), early("ones", [P, P], BF16)
        hscan, base = early("hscan", [P, 2, NB]), early("base", [P, 2, NB])
        junk = [early(f"junk{r}", [P, NB]) for r in range(2)]
        minus = early("minus", [1, 4], I32)
        pb = [early(f"pb{o}", [EB, T, P, 4], I32) for o in range(3)]
        bsame, bw, bsrc, bdst, bout = (early(n, [EB, T, P]) for n in ("bsame", "bw", "bsrc", "bdst", "bout"))

        pay = [early(f"pay{s}", [P, T, 4], I32) for s in range(SL)]
        dig4i = [early(f"dig4i{s}", [P, T], I32) for s in range(SL)]
        dig4 = [early(f"dig4_{s}", [P, T]) for s in range(SL)]
        pos4 = [early(f"pos4_{s}", [P, T]) for s in range(SL)]
        prep_ctx.close()

        def slots(name, shape, dt=F32):
            return [sb(f"{name}{s}", shape, dt) for s in range(SL)]

        gat = slots("gat", [P, T, ZW])
        fwB, ffB = slots("fwB", [P, 2, G]), slots("ffB", [P, 2, G])
        fB, wB, f2B, fmB = ([t[:, k, :] for t in pair] for pair in (fwB, ffB) for k in range(2))
        msg, zT = slots("msg", [P, G]), slots("zT", [P, G])
        zE = slots("zE", [P, T, ZW])
        xT = slots("xT", [P, T, P])
        xc = slots("xc", [P, T, 3, P])
        x1, x2, x3 = ([c[:, :, k, :] for c in xc] for k in range(3))
        x1T = slots("x1T", [P, G])
        hT = [slots(f"hT{c}_", [P, G]) for c in range(HC)]
        t2, x2T, x4 = slots("t2", [P, T, P]), slots("x2T", [P, T, P]), slots("x4", [P, T, P])
        zin = [slots(f"zin{k}_", [P, T, P]) for k in range(3)]
        mbuf = slots("mbuf", [P, G + 1])
        lns = [(slots(f"ln{k}st", [P, T, 6]), slots(f"ln{k}mv", [P, T, 2]), slots(f"ln{k}sd", [P, T]),
                slots(f"ln{k}rs", [P, T]), slots(f"ln{k}nm", [P, T])) for k in range(1, 5)]
        rden = slots("rden", [P, 2 * T])
        dmax = slots("dmax", [P, 2 * T])

        def flat(t):
            return t[:, :, :].rearrange("p t f -> p (t f)")

        def flat(t):
            return t[:, :, :].rearrange("p t f -> p (t f)")

        att, mnt, atr = ([flat(a) for a in z] for z in zin)
        invB = hT[0]
        x2d = fB
        xs, qT, prod, dlt, dec, elt = x1T, hT[0], hT[1], att, mnt, atr
        aw, av, den, agg, aggn, own = wB, f2B, zT, msg, x2T, xT

        def epos(g):
            return bass.ds(g * G, G)

        def at(eng, name, s, count):
            count = count + BASE.get(name, 0)
            if isinstance(count, int) and count <= 0:
                return
            eng.wait_ge(S(name, s), count if by_slot(name) else count * SL + (s + 1 - SL))
            if eng.engine == mybir.EngineType.SP:
                eng.sem_inc(S("go_sp"), 1)

        def ready(eng, name, s, i, n=1):
            at(eng, name, s, (i + 1) * n)

        def reuse(eng, name, s, i, n=1):
            at(eng, name, s, i * n)

        def prior(eng, name, s, i):
            if s > 0:
                at(eng, name, s - 1, i + 1)
            else:
                at(eng, name, SL - 1, i)

        def prepared(eng):
            eng.wait_ge(S("st_rows"), 16 * 7)
            eng.wait_ge(S("st_tab"), 16 * 10)
            eng.wait_ge(S("zeroed"), 16 * (SL * EI + 1))

        def steps(eng, n, *stages):
            def iteration(i):
                for s in range(SL):
                    for stage, lag in stages:
                        back = (s - lag) // SL
                        if not isinstance(i, int) or 0 <= i + back < n:
                            stage(i + back, (s - lag) % SL)

            most = max(lag for _, lag in stages)
            apart = 2 if most else 1
            for i in range(apart):
                iteration(i)
            with eng.Fori(apart, n) as i:
                iteration(i)
            for i in range(n, n + -(-most // SL)):
                iteration(i)

        def all_slots(eng, name, count):
            if by_slot(name):
                for s in range(SL):
                    at(eng, name, s, count)
            else:
                at(eng, name, SL - 1, count)

        block = ctx.enter_context(nc.Block())
        ctx.enter_context(nc.allow_non_contiguous_dma(reason="index tables of four words per partition"))

        def seq(k, i):
            return i + k * EI

        def ci(kind, i):
            return i + {"node": 0, "s": NI, "d": NI + EI}[kind]

        def li(kind, k, i):
            return i + {"node": 0, "s": NI, "d": NI + EI, "att": NI + (EI if k == 2 else 0), "fin": NI + EI}[kind]

        def alone(kind, k):
            return k == 3 and kind != "fin"

        def tile_no(k, i, s, j):
            return (i * SL + s) * T + (k * EC + j)

        def tiles_done(eng, name, count):
            if isinstance(count, int) and count <= 0:
                return
            eng.wait_ge(S(name), count)

        @block.sync
        def _(sp):
            def table_store(name):
                sp.dma_start(TAB[name], tabs[name][:, :]).then_inc(S("st_tab"), 16)

            for t, a in ((fsrc, src_flat), (fdst, dst_flat[1:E_PAD + 1]), (fw, w_flat)):
                sp.dma_start(t[:, :], a.rearrange("(p c) -> p c", p=P)).then_inc(S("ld_flat"), 16)
            sp.dma_start(gsrc[:, :], src_g).then_inc(S("ld_gsrc"), 16)
            sp.dma_start(dstp[:, :], dst_flat[0:E_PAD].rearrange("(p c) -> p c", p=P)).then_inc(S("ld_prep"), 16)
            sp.dma_start(dstc[:, :], dst_flat[1:E_PAD + 1].rearrange("(p c) -> p c", p=P)).then_inc(S("ld_prep"), 16)
            sp.dma_start(dstn[:, :], dst_flat[2:E_PAD + 2].rearrange("(p c) -> p c", p=P)).then_inc(S("ld_prep"), 16)
            for t, a in ((gdst, dst_g), (gdn, dnext_g)):
                sp.dma_start(t[:, :], a).then_inc(S("ld_prep"), 16)
            for t, a in ((W0I[:, :, :], W0.rearrange("(k p) n -> p k n", p=P)),
                         (W1x[:, :], W1[0:P, :]),
                         (W1u[:, :], W1[P + 3 * AF:P + 3 * AF + UF, :]),
                         (ucol[:, :], u[0:1, :].rearrange("a f -> f a")),
                         (b1c[:, :], b1.rearrange("(c p) -> p c", p=P)),
                         (W2s[:, :, :], W2.rearrange("(c p) n -> p c n", p=P)),
                         (Wqs[:, :], Wq), (Wks[:, :], Wk), (Wvs[:, :], Wv), (WsI[:, :], Ws),
                         (bqc[:, :], bq.rearrange("(p a) -> p a", a=1)),
                         (bkc[:, :], bk.rearrange("(p a) -> p a", a=1)),
                         (bvc[:, :], bv.rearrange("(p a) -> p a", a=1)),
                         (brow[:, 0, :], b0.rearrange("(a p) -> a p", a=1)),
                         (brow[:, 1, :], b2.rearrange("(a p) -> a p", a=1)),
                         (brow[:, 2, :], bs.rearrange("(a p) -> a p", a=1))):
                sp.dma_start(t, a).then_inc(S("ld_const"), 16)
            sp.wait_ge(S("init_w1"), 1)
            for t, a in ((W1a[0:AF, :], W1[P:P + AF, :]),
                         (W1a[AM:AK, :], W1[P + AF:P + 2 * AF, :]),
                         (W1m[0:AF, :], W1[P + 2 * AF:P + 3 * AF, :])):
                sp.dma_start(t, a).then_inc(S("ld_const"), 16)
            sp.wait_ge(S("payload"), 3)
            sp.dma_start(PAY[1:E_PAD + 1, :].rearrange("(p c) w -> p (c w)", p=P),
                         payl[:, :, :].rearrange("p c w -> p (c w)")).then_inc(S("st_pay"), 16)
            sp.wait_ge(S("minus"), 1)
            for r in (0, E_PAD + 1):
                sp.dma_start(PSRC[r:r + 1, :], minus[:, :]).then_inc(S("st_pay"), 16)
            sp.wait_ge(S("init_zero"), 1)
            sp.dma_start(Z2E[0:1, :], zeros[0:1, 0:P]).then_inc(S("zeroed"), 16)
            sp.wait_ge(S("cnt_local"), 2)
            sp.dma_start(cols_d[0:1, :].rearrange("a p -> p a"), cntl[:, EC - 1:EC]).then_inc(S("carry"), 16)
            sp.dma_start(cols_d[1:2, :].rearrange("a p -> p a"), allsame[:, EC - 1:EC]).then_inc(S("carry"), 16)
            sp.wait_ge(S("carry"), 32)
            sp.dma_start(crow[:, 0:2, :], cols_d[0:2, :].rearrange("(o a) p -> o a p", o=1)).then_inc(S("carry_row"), 16)
            sp.wait_ge(S("carry_scan"), 1)
            sp.dma_start(cols_d[2:3, 1:P], crow[0:1, 2, 0:P - 1]).then_inc(S("carry_out"), 16)
            sp.dma_start(cols_d[2:3, 0:1], zeros[0:1, 0:1]).then_inc(S("carry_out"), 16)
            sp.wait_ge(S("carry_out"), 32)
            sp.dma_start(ccol[:, :], cols_d[2:3, :].rearrange("a p -> p a")).then_inc(S("carry_col"), 16)
            sp.wait_ge(S("flags"), 1)
            for nm, t in (("same", same), ("samem", samem), ("notlast", notlast), ("last", last)):
                sp.dma_start(ROWS[nm].rearrange("a (p c) -> (a p) c", p=P), t[:, :]).then_inc(S("st_rows"), 16)
            sp.wait_ge(S("inv"), 1)
            sp.dma_start(ROWS["inv"].rearrange("a (p c) -> (a p) c", p=P), inv[:, :]).then_inc(S("st_rows"), 16)
            sp.wait_ge(S("d_tabs"), 6)
            for nm in ("d_x1", "d_x2_out", "d_x3_out", "d_out", "d_x2s"):
                table_store(nm)
            sp.wait_ge(S("bias_split"), 3)
            for k in range(3):
                sp.dma_start(bias3[k:k + 1, :, :], bsp[0:1, k, :, :]).then_inc(S("ld_bias"), 16)

            sp.wait_ge(S("hist"), 1)
            for k in range(2):
                sp.dma_start(HIST[k:k + 1, :].rearrange("o (a b) -> (o a) b", b=HB),
                             hist_s[k * HA:(k + 1) * HA, k * HB:(k + 1) * HB]).then_inc(S("st_hist"), 16)
            sp.wait_ge(S("st_hist"), 32)
            sp.dma_start(hist[:, :, :].rearrange("p k n -> p (k n)"),
                         HIST.rearrange("(o k) n -> o (k n)", o=1).to_broadcast([P, 2 * NB])).then_inc(S("ld_hist"), 16)

            sp.wait_ge(S("st_pay"), 48)
            for k in (1, 2):
                table = {1: PAY, 2: PLOW}[k]
                if k == 2:
                    all_slots(sp, "placed", EI * 64)

                def pay_load(i, s):
                    at(sp, "placed", s, i * 64 + (k - 1) * EI * 64)
                    sp.dma_start(pay[s][:, :, :], table[bass.ds((i * SL + s) * G + 1, G), :]
                                 .rearrange("(t p) w -> p t w", p=P)).then_inc(S("ld_pay", s), 16)

                def zero_store(i, s):
                    sp.dma_start(Z1N[bass.ds((i * SL + s) * 2 * G, 2 * G), :].rearrange("(p a) w -> p (a w)", p=P),
                                 zeros[:, 0:2 * T * ZW]).then_inc(S("zeroed"), 16)

                steps(sp, EI, (pay_load, 0), *([(zero_store, 0)] if k == 1 else []))

            all_slots(sp, "placed", 2 * EI * 64)
            for o in range(3):
                sp.dma_start(pb[o][:, :, :, :].rearrange("p b n w -> p b (n w)"),
                             PSRC[o:o + E_PAD, :].rearrange("(b p n) w -> p b (n w)", b=T, p=EB)
                             ).then_inc(S("ld_blocks"), 16)
            sp.wait_ge(S("s_rows"), 2)
            for nm, t in (("s_same", bsame), ("s_w", bw)):
                sp.dma_start(ROWS[nm].rearrange("a (b p n) -> p (a b) n", b=T, p=EB), t[:, :, :]
                             ).then_inc(S("st_rows"), 16)
            sp.wait_ge(S("s_tabs"), 5)
            for nm in ("s_dst", "s_src", "s_out", "s_x3d", "s_x3s"):
                table_store(nm)
            prepared(sp)

            def pair_load(t, pair, g, sem):
                sp.dma_start(t[:, :, :], PAIRS[pair][:, epos(g)].rearrange("(o k) n -> o k n", o=1
                                                                           ).to_broadcast([P, 2, G])).then_inc(sem, 16)

            def row_load(t, row, g, sem, first=0, n=P):
                sp.dma_start(t[first:first + n, :], row[0:1, epos(g)].to_broadcast([n, G])).then_inc(sem, 16)

            def index_load(t, name, g, sem):
                sp.dma_start(t[:, :], TAB[name][:, bass.ds(g * T, T)]).then_inc(sem, 16)

            def gather_index(k, name, rev=False):
                def stage(i, s):
                    at(sp, "gathered", s, seq(k, i) * 64)
                    index_load(idx[s], name, edge_group(i, s, rev), S("ld_idx", s))
                return stage

            def scatter_index(k, name, rev=False):
                def stage(i, s):
                    at(sp, "scattered", s, seq(k, i) * 64)
                    index_load(sct[s], name, edge_group(i, s, rev), S("ld_sct", s))
                return stage

            def edge_group(i, s, rev):
                return (SL * EI - 1 - s) - i * SL if rev else i * SL + s

            def spmm_rows(k):
                def stage(i, s):
                    at(sp, "scanned", s, seq(k, i))
                    pair_load(fwB[s], ("s_same", "s_w"), i * SL + s, S("ld_row", s))
                return stage

            def z_store(k):
                def stage(i, s):
                    g = i * SL + s
                    ready(sp, "scanned", s, seq(k, i))
                    sp.dma_start(ZT[k][:, epos(g)], zT[s][:, :]).then_inc(S("st_zT", s), 16)
                    if k == 1:
                        ready(sp, "z_rows", s, seq(1, i))
                        sp.dma_start(Z2E[bass.ds(g * G + 1, G), :].rearrange("(t p) f -> p t f", p=P),
                                     zE[s][:, :, 0:P]).then_inc(S("st_z2", s), 16)
                return stage

            def rows_of(table, g):
                return table[bass.ds(g * G, G), :].rearrange("(p t) f -> p t f", t=T)

            for k in range(2):
                def node_load(i, s):
                    c = i + DPP * k
                    reuse(sp, "mm1", s, c)
                    sp.dma_start(flat(xT[s]), x_fm[:, bass.ds((c * SL + s) * G, G)]).then_inc(S("ld_x", s), 16)

                def x12_store(i, s):
                    c = i + DPP * k
                    ready(sp, "ln2_out", s, c)
                    sp.dma_start(rows_of(XT, c * SL + s)[:, :, 0:2 * P],
                                 xc[s][:, :, 0:2, :].rearrange("p t k f -> p t (k f)")).then_inc(S("st_x12_", s), 16)

                def x3_store(i, s):
                    c = i + DPP * k
                    ready(sp, "ln3_out", s, c)
                    sp.dma_start(rows_of(XT, c * SL + s)[:, :, 2 * P:3 * P], x3[s]).then_inc(S("st_x3_", s), 16)

                def x4_store(i, s):
                    c = i + DPP * k
                    ready(sp, "ln4_out", s, c)
                    sp.dma_start(rows_of(out, c * SL + s), x4[s][:, :, :]).then_inc(S("st_x4", s), 16)

                stages = [(node_load, 0), (gather_index(k, "s_dst"), 0), (spmm_rows(k), 0)]
                if k == 0:
                    stages += [(scatter_index(0, "s_out"), 1)]
                steps(sp, EI, *stages, (z_store(k), 3), (x12_store, 4), (x3_store, 5), (x4_store, 6))

            sp.wait_ge(S("s_ztab"), 1)
            table_store("s_z")
            sp.wait_ge(S("st_tab"), 16 * 11)

            def attr_load(i, s):
                g = i * SL + s
                reuse(sp, "attr_mean", s, i)
                sp.dma_start(atr[s][0:AK, :], attr_fm[:, epos(g)]).then_inc(S("ld_attr", s), 16)
                row_load(f2B[s], ROWS["same"], g, S("ld_attr", s), 0, AF)
                row_load(fmB[s], ROWS["samem"], g, S("ld_attr", s), AM, AF)
                row_load(invB[s], ROWS["inv"], g, S("ld_attr", s), 0, AF)

            def attr_store(i, s):
                g = i * SL + s
                ready(sp, "attr_mean", s, i)
                sp.dma_start(ATT[:, epos(g)], att[s][0:AK, :]).then_inc(S("st_att", s), 16)
                sp.dma_start(MNT[:, epos(g)], mnt[s][0:AF, :]).then_inc(S("st_att", s), 16)

            steps(sp, EI, (gather_index(2, "s_z"), 0), (spmm_rows(2), 0), (attr_load, 0),
                  (z_store(2), 4), (attr_store, 4))

            all_slots(sp, "st_zT", 3 * EI * 16)
            all_slots(sp, "st_att", EI * 32)

            def z_load(i, s):
                reuse(sp, "mm1", s, ci("s", i))
                for k in range(3):
                    sp.dma_start(flat(zin[k][s]), ZT[k][:, epos(i * SL + s)]).then_inc(S("ld_z", s), 16)

            steps(sp, EI, (gather_index(3, "s_src"), 0), (z_load, 0), (scatter_index(1, "s_out"), 3))

            all_slots(sp, "mm1", NI + EI)

            def att_load(i, s):
                g = edge_group(i, s, True)
                reuse(sp, "hidden", s, ci("d", i))
                sp.dma_start(att[s][0:AK, :], ATT[:, epos(g)]).then_inc(S("ld_att", s), 16)
                sp.dma_start(mnt[s][0:AF, :], MNT[:, epos(g)]).then_inc(S("ld_att", s), 16)
                reuse(sp, "x2d", s, i)
                pair_load(ffB[s], ("last", "notlast"), g, S("ld_last", s))

            def x2d_store(i, s):
                ready(sp, "x2d", s, i)
                sp.dma_start(X2DT[:, epos(edge_group(i, s, True))], x2d[s][:, :]).then_inc(S("st_x2d", s), 16)

            steps(sp, EI, (gather_index(4, "d_x1", True), 0), (att_load, 0), (scatter_index(2, "d_x2_out", True), 2),
                  (x2d_store, 5))

            all_slots(sp, "st_x2d", 16 * EI)

            def x2d_load(i, s):
                reuse(sp, "skip_e", s, i)
                reuse(sp, "decayed", s, i)
                sp.dma_start(x2d[s][:, :], X2DT[:, epos(i * SL + s)]).then_inc(S("ld_x2d", s), 16)
                row_load(fmB[s], ROWS["samem"], i * SL + s, S("ld_x2d", s))

            def out_index(i, s):
                reuse(sp, "scattered2", s, i, 64)
                index_load(idx2[s], "d_out", i * SL + s, S("ld_idx2", s))

            steps(sp, EI, (gather_index(5, "d_x2s"), 0), (x2d_load, 0), (scatter_index(3, "d_x3_out"), 3), (out_index, 4))

            all_slots(sp, "skip_e", EI)
            all_slots(sp, "agg", EI)
            all_slots(sp, "scattered2", EI * 64)

            def own_index(i, s):
                reuse(sp, "gathered2", s, i, 64)
                index_load(idx2[s], "s_x3s", i * SL + s, S("ld_idx2", s))

            steps(sp, EI, (gather_index(6, "s_x3d"), 0), (spmm_rows(3), 0), (own_index, 0), (scatter_index(4, "s_out"), 1))

        @block.gpsimd
        def _(pool):
            pool.iota(enum_i[:, :], pattern=[[P, EC]], base=1, channel_multiplier=1).then_inc(S("enum_i"), 1)
            pool.memset(ident[:, :], 0.0).then_inc(S("ident0"), 1)
            pool.wait_ge(S("ident0"), 1)
            pool.affine_select(out=ident[:, :], in_=ident[:, :], compare_op=ALU.not_equal, fill=1.0, base=0,
                               pattern=[[-1, P]], channel_multiplier=1).then_inc(S("ident"), 1)

            pool.iota(buckets_i[:, :], pattern=[[1, NB]], base=0, channel_multiplier=0).then_inc(S("enum_i"), 1)
            pool.memset(before[:, :], 1.0).then_inc(S("ident0"), 1)
            pool.memset(rest[:, :], 1.0).then_inc(S("ident0"), 1)
            pool.memset(ones[:, :], 1.0).then_inc(S("ident0"), 1)
            pool.memset(minus[:, :], -1).then_inc(S("minus"), 1)
            pool.wait_ge(S("ident0"), 4)
            pool.affine_select(out=before[:, :], in_=before[:, :], compare_op=ALU.is_gt, fill=0.0, base=0,
                               pattern=[[1, P]], channel_multiplier=-1).then_inc(S("triangles"), 1)
            pool.affine_select(out=rest[:, :], in_=rest[:, :], compare_op=ALU.is_ge, fill=0.0, base=0,
                               pattern=[[-1, P]], channel_multiplier=1).then_inc(S("triangles"), 1)

            def gather(table, width, tile, index, sem):
                pool.sem_inc(S("go"), 1)
                for t in range(T):
                    pool.indirect_dma_start(
                        out=tile[:, t, 0:width], out_offset=None, in_=table,
                        in_offset=bass.IndirectOffsetOnAxis(ap=index[:, t:t + 1], axis=0)).then_inc(sem, 16)

            def scatter(table, rows, index, sem):
                pool.sem_inc(S("go"), 1)
                for t in range(T):
                    pool.indirect_dma_start(
                        out=table, out_offset=bass.IndirectOffsetOnAxis(ap=index[:, t:t + 1], axis=0),
                        in_=rows[t], in_offset=None,
                        bounds_check=table.shape[0] - 1, oob_is_err=False).then_inc(sem, 16)

            for k in (1, 2):
                def place(i, s):
                    at(pool, "ranked", s, i + ((k - 1) * EI + 1))
                    scatter(PLOW if k == 1 else PSRC, [pay[s][:, t, :] for t in range(T)], idx[s], S("placed", s))

                steps(pool, EI, (place, 0))

            prepared(pool)

            def z_gather(k):
                def stage(i, s):
                    at(pool, "turned", s, seq(k, i))
                    if k == 1:
                        reuse(pool, "coded", s, i)
                    ready(pool, "ld_idx", s, seq(k, i), 16)
                    gather([x_rows, Z1N, Z2E, x_rows][k], ZW if k == 1 else P, gat[s], idx[s], S("gathered", s))
                return stage

            def z_scatter(i, s):
                ready(pool, "ld_sct", s, i, 16)
                ready(pool, "z_rows", s, i)
                ready(pool, "numbered", s, i)
                scatter(Z1N, [zE[s][:, t, :] for t in range(T)], sct[s], S("scattered", s))

            steps(pool, EI, (z_gather(0), 0), (z_scatter, 3))
            all_slots(pool, "scattered", EI * 64)
            steps(pool, EI, (z_gather(1), 0))
            all_slots(pool, "st_z2", EI * 16)
            all_slots(pool, "coded", EI)
            steps(pool, EI, (z_gather(2), 0))

            def source_scatter(i, s):
                ready(pool, "ld_sct", s, seq(1, i), 16)
                ready(pool, "ln3_out", s, ci("s", i))
                scatter(XT, [xc[s][:, t, :, :].rearrange("p k f -> p (k f)") for t in range(T)], sct[s],
                        S("scattered", s))

            all_slots(pool, "st_x12_", NI * 16)
            all_slots(pool, "st_x3_", NI * 16)
            steps(pool, EI, (z_gather(3), 0), (source_scatter, 5))

            all_slots(pool, "scattered", 2 * EI * 64)
            all_slots(pool, "turned", 4 * EI)

            def dst_gather(i, s):
                at(pool, "x1_turned", s, ci("d", i))
                at(pool, "t2", s, ci("d", i))
                ready(pool, "ld_idx", s, seq(4, i), 16)
                gather(XT3, P, gat[s], idx[s], S("gathered", s))

            def dst_scatter(i, s):
                ready(pool, "ld_sct", s, seq(2, i), 16)
                ready(pool, "ln2_out", s, ci("d", i))
                scatter(XT3, [x2[s][:, t, :] for t in range(T)], sct[s], S("scattered", s))

            steps(pool, EI, (dst_gather, 0), (dst_scatter, 4))

            all_slots(pool, "scattered", 3 * EI * 64)
            all_slots(pool, "x1_turned", NI + 2 * EI)
            all_slots(pool, "t2", NI + 2 * EI)
            all_slots(pool, "st_x4", 16 * NI)

            def att_gather(i, s):
                at(pool, "turned", s, seq(4, i))
                ready(pool, "ld_idx", s, seq(5, i), 16)
                gather(XT3, P, gat[s], idx[s], S("gathered", s))

            def x3_scatter(i, s):
                ready(pool, "ld_sct", s, seq(3, i), 16)
                ready(pool, "ln3_out", s, li("att", 2, i))
                scatter(XT3, [x3[s][:, t, :] for t in range(T)], sct[s], S("scattered", s))

            def out_scatter(i, s):
                ready(pool, "ld_idx2", s, i, 16)
                ready(pool, "ln4_out", s, li("att", 3, i))
                scatter(out, [x4[s][:, t, :] for t in range(T)], idx2[s], S("scattered2", s))

            steps(pool, EI, (att_gather, 0), (x3_scatter, 5), (out_scatter, 6))

            all_slots(pool, "scattered", 4 * EI * 64)
            all_slots(pool, "scattered2", EI * 64)

            def fin_gather(i, s):
                at(pool, "turned", s, seq(5, i))
                ready(pool, "ld_idx", s, seq(6, i), 16)
                gather(XT3, P, gat[s], idx[s], S("gathered", s))
                reuse(pool, "fin_scaled", s, i)
                ready(pool, "ld_idx2", s, seq(1, i), 16)
                gather(XT3, P, own[s], idx2[s], S("gathered2", s))

            def fin_scatter(i, s):
                ready(pool, "ld_sct", s, seq(4, i), 16)
                ready(pool, "ln4_out", s, li("fin", 3, i))
                scatter(out, [x4[s][:, t, :] for t in range(T)], sct[s], S("scattered", s))

            steps(pool, EI, (fin_gather, 0), (fin_scatter, 3))
            all_slots(pool, "scattered", 5 * EI * 64)

        @block.tensor
        def _(pe):
            pe.wait_ge(S("ident"), 1)
            pe.wait_ge(S("triangles"), 2)

            def count(i, s):
                for j in range(T):
                    if j == 0:
                        at(pe, "parts_hot", s, i + 1)
                    first = isinstance(i, int) and i + s + j == 0
                    mm = pe.matmul(bT1[0:2 * HA, 0, 0:2 * HB], oha[s][:, j, :, :].rearrange("p k a -> p (k a)"),
                                   ohb[s][:, j, :, :].rearrange("p k b -> p (k b)"), start=first, stop=False,
                                   skip_group_check=True)
                mm.then_inc(S("counted"), 1)

            steps(pe, EI, (count, 0))

            for k in (1, 2):
                pair = (bH0, bH1) if k == 1 else (bMLP, bSK)
                pe.wait_ge(S("bases"), 2)
                for b in range(2):
                    pe.matmul(pair[b][:, :, :], ident[:, :], base[:, k - 1, :], start=True, stop=False,
                              skip_group_check=True)

                def rank(i, s):
                    first = isinstance(i, int) and i + s == 0
                    for j in range(T):
                        bk_ = pair[j % 2]
                        tiles_done(pe, "one_hot", tile_no(k - 1, i, s, j + 1))
                        if not first or j >= 2:
                            tiles_done(pe, "ranked_tile", tile_no(k - 1, i, s, j - 1))
                            pe.matmul(bk_[:, :, :], rest[:, :], oh[(j - 2) % 4][:, :], start=False, stop=False,
                                      skip_group_check=True)
                        if not first or j >= 1:
                            pe.matmul(bk_[:, :, :], ones[:, :], oh[(j - 1) % 4][:, :], start=False, stop=False,
                                      skip_group_check=True)
                        pe.matmul(bk_[:, :, :], before[:, :], oh[j][:, :], start=False, stop=False,
                                  skip_group_check=True).then_inc(S("before"), 1)

                steps(pe, EI, (rank, 0))

            pe.wait_ge(S("blocks"), 3)
            for a, bk_ in ((bsrc, bH0), (bdst, bH1), (bout, bMLP)):
                for b in range(T):
                    mm = pe.transpose(bk_[:, :, :].rearrange("p t f -> p (t f)")[:, b * EB:(b + 1) * EB],
                                      a[:, b, :], ident[0:EB, 0:EB])
                mm.then_inc(S("s_turned"), 1)

            pe.wait_ge(S("ld_const"), 16 * 19)
            for c in range(HC):
                mm = pe.matmul(bT1[:, c, 0:1], W1u[:, c * P:(c + 1) * P], ucol[:, :], start=True, stop=True)
            mm.then_inc(S("u_part"), 1)
            pe.wait_ge(S("b1u"), 1)
            pe.wait_ge(S("s_tabs"), 5)
            pe.wait_ge(S("W_ready"), 2)
            pe.wait_ge(S("ld_bias"), 48)
            pe.wait_ge(S("consts"), 1)

            def turn(dst, tiles):
                for t in range(T):
                    mm = pe.transpose(dst[:, t, :], tiles[t], ident[:, :])
                return mm

            def z_turn(k):
                def stage(i, s):
                    at(pe, "gathered", s, (seq({4: 5, 5: 6}.get(k, k), i) + 1) * 64)
                    if k == 3:
                        prior(pe, "x_src", s, i)
                    elif k == 4:
                        prior(pe, "att_src", s, i)
                    else:
                        prior(pe, "weighted", s, seq(min(k, 3), i))
                    turn(bIN, [gat[s][:, t, 0:P] for t in range(T)]).then_inc(S("turned", s), 1)
                return stage

            def z_back(k):
                def stage(i, s):
                    ready(pe, "scanned", s, seq(k if k < 2 else 3, i))
                    if k < 2:
                        prior(pe, "z_rows", s, seq(k, i))
                    else:
                        prior(pe, "fin_sum", s, i)
                    turn(bBK, [zT[s][:, t * P:(t + 1) * P] for t in range(T)]).then_inc(S("back", s), 1)
                return stage

            def chain_a(kind, i, s):
                c = ci(kind, i)
                prior(pe, "ln1_out", s, c)
                if kind == "s":
                    ready(pe, "x_src", s, i)
                    ready(pe, "ld_z", s, i, 48)
                else:
                    ready(pe, "ld_x", s, i, 16)
                bias(bT1, 0)
                for t in range(T):
                    mm = pe.matmul(bT1[:, t, :], xT[s][:, t, :], W0I[:, 0, :], start=False,
                                   stop=kind == "node", skip_group_check=True)
                    if kind == "s":
                        for k in range(3):
                            mm = pe.matmul(bT1[:, t, :], zin[k][s][:, t, :], W0I[:, k + 1, :], start=False,
                                           stop=k == 2, skip_group_check=True)
                mm.then_inc(S("mm1", s), 1)

            def bias(bank_, k):
                pe.matmul(bank_[:, :, :], ones3[:, :], bias3[:, k:k + 1, :].to_broadcast([3, T, P]),
                          start=True, stop=False, skip_group_check=True)

            def chain_b1(kind, i, s):
                c = ci(kind, i)
                if kind == "d":
                    at(pe, "gathered", s, (seq(4, i) + 1) * 64)
                    prior(pe, "x1T", s, c)
                    turn(bIN, [gat[s][:, t, 0:P] for t in range(T)]).then_inc(S("x1_turned", s), 1)
                else:
                    ready(pe, "ln1_out", s, c)
                    turn_shared(c, s, 3, "x2T")
                    turn(bTR, [x1[s][:, t, :] for t in range(T)]).then_inc(S("x1_turned", s), 1)

            def turn_shared(c, s, back, name):
                d = (s - back) // SL
                at(pe, name, (s - back) % SL, c + d + 1)

            def chain_b2(kind, i, s):
                c = ci(kind, i)
                ready(pe, "x1T", s, c)
                prior(pe, "relu", s, c)
                if kind == "d":
                    ready(pe, "ld_att", s, i, 32)
                for h in range(HC):
                    cols = slice(h * P, (h + 1) * P)
                    mm = pe.matmul(bH[h][:, :, :], W1x[:, cols], x1T[s][:, :], start=True, stop=kind != "d")
                    if kind == "d":
                        pe.matmul(bH[h][:, :, :], W1a[0:AK, cols], att[s][0:AK, :], start=False, stop=False)
                        mm = pe.matmul(bH[h][:, :, :], W1m[0:AF, cols], mnt[s][0:AF, :], start=False, stop=True)
                mm.then_inc(S("hidden", s), 1)

            def chain_c(kind, i, s):
                c = ci(kind, i)
                ready(pe, "relu", s, c)
                prior(pe, "t2", s, c)
                bias(bMLP, 1)
                for t in range(T):
                    for h in range(HC):
                        mm = pe.matmul(bMLP[:, t, :], hT[h][s][:, t * P:(t + 1) * P], W2s[:, h, :], start=False,
                                       stop=h == HC - 1, skip_group_check=True)
                mm.then_inc(S("mlp", s), 1)

            def chain_d1(kind, i, s):
                c = ci(kind, i)
                ready(pe, "ln2_out", s, c)
                if kind == "d":
                    prior(pe, "x2sel", s, i)
                else:
                    ahead = (s + 2) // SL
                    last = {"node": EI, "s": EI}[kind]
                    if isinstance(i, int) and (i * SL + s) % (last * SL) + 2 >= last * SL:
                        at(pe, "x1T", SL - 1, c - i % last + last)
                    else:
                        at(pe, "x1T", (s + 2) % SL, c + ahead + 1)
                turn(bTR, [x2[s][:, t, :] for t in range(T)]).then_inc(S("x2_turned", s), 1)

            def chain_d2(kind, i, s):
                c = ci(kind, i)
                ready(pe, "x2T", s, c)
                prior(pe, "ln3_out", s, c)
                skip(x2T[s], bSK, S("skip", s))

            def skip(lhs, dst, sem):
                bias(dst, 2)
                for t in range(T):
                    mm = pe.matmul(dst[:, t, :], lhs[:, t, :], WsI[:, :], start=False, stop=True,
                                   skip_group_check=True)
                mm.then_inc(sem, 1)

            def of(kind, stage, first=0):
                return lambda i, s: stage(kind, i + first, s)

            for k in range(2):
                c = DPP * k
                all_slots(pe, "x2T", c)
                steps(pe, EI, (of("node", chain_b1, c), 1), (of("node", chain_a, c), 0),
                      (of("node", chain_b2, c), 1), (of("node", chain_d1, c), 3), (of("node", chain_c, c), 2),
                      (z_turn(k), 0), (of("node", chain_d2, c), 3), (z_back(k), 1))

            steps(pe, EI, (z_turn(2), 0))
            all_slots(pe, "weighted", 3 * EI)
            all_slots(pe, "x2T", NI)

            steps(pe, EI, (of("s", chain_b1), 2), (of("s", chain_a), 1), (of("s", chain_b2), 2),
                  (of("s", chain_d1), 4), (of("s", chain_c), 3), (z_turn(3), 0), (of("s", chain_d2), 4))
            all_slots(pe, "x2T", NI + EI)
            all_slots(pe, "x_src", EI)

            steps(pe, EI, (of("d", chain_b1), 0), (of("d", chain_c), 2), (of("d", chain_d1), 3),
                  (of("d", chain_b2), 1))

            all_slots(pe, "ln1_out", NI + EI)
            all_slots(pe, "ln3_out", NI + EI)
            all_slots(pe, "t2", NI + 2 * EI)
            all_slots(pe, "relu", NI + 2 * EI)
            all_slots(pe, "x2sel", EI)
            all_slots(pe, "x1T", NI + 2 * EI)

            def att_q(i, s):
                ready(pe, "ld_x2d", s, i, 32)
                prior(pe, "q_out", s, i)
                pe.matmul(bT1[:, :, :], Wqs[:, :], x2d[s][:, :], start=True, stop=True).then_inc(S("q_mm", s), 1)

            def att_k(i, s):
                ready(pe, "att_src", s, i)
                prior(pe, "qk", s, i)
                pe.matmul(bMLP[:, :, :], Wks[:, :], xs[s][:, :], start=True, stop=True).then_inc(S("k_mm", s), 1)

            def att_v(i, s):
                prior(pe, "weighted_v", s, i)
                pe.matmul(bH0[:, :, :], Wvs[:, :], xs[s][:, :], start=True, stop=True).then_inc(S("v_mm", s), 1)

            def att_alpha(i, s):
                ready(pe, "qk", s, i)
                prior(pe, "centred", s, i)
                pe.matmul(bSK[:, :, :], heads[:, :], prod[s][:, :], start=True, stop=True).then_inc(S("alpha", s), 1)

            def att_base(i, s):
                prior(pe, "t3", s, i)
                skip(x2d[s][:, :].rearrange("p (t f) -> p t f", t=T), bBK, S("skip_e", s))

            def att_back(i, s):
                ready(pe, "agg", s, i)
                prior(pe, "agg_norm", s, i)
                turn(bTR, [agg[s][:, t * P:(t + 1) * P] for t in range(T)])
                for t in range(T):
                    mm = pe.matmul(bH1[:, 0, 2 * t:2 * t + 2], den[s][:, t * P:(t + 1) * P], hsel[:, :],
                                   start=True, stop=True, skip_group_check=True)
                mm.then_inc(S("agg_turned", s), 1)

            steps(pe, EI, (z_turn(4), 0), (att_q, 0), (att_alpha, 1), (att_v, 2), (att_base, 3), (att_k, 0),
                  (att_back, 3))
            all_slots(pe, "att_src", EI)
            all_slots(pe, "t3", EI)

            steps(pe, EI, (z_turn(5), 0), (z_back(2), 1))

        @block.scalar
        def _(act):
            act.wait_ge(S("u_part"), 1)
            for c in range(HC):
                a = act.activation(b1u[:, c:c + 1], bT1[:, c, 0:1], ACT.Identity, bias=b1c[:, c:c + 1])
            a.then_inc(S("b1u"), 1)
            act.wait_ge(S("b1u"), 1)
            act.wait_ge(S("consts"), 1)

            def evac(dst, src, sem):
                act.copy(dst, src).then_inc(sem, 1)

            def std(kind, k, first=0):
                def stage(i, s):
                    c = li(kind, k, i + first)
                    _, mv, sd, _, _ = lns[k]
                    ready(act, f"variance{k}", s, c)
                    act.activation(sd[s][:, :], mv[s][:, :, 1], ACT.Sqrt, bias=epsc[:, :],
                                   scale=1.25 ** 2 if alone(kind, k) else 1.0).then_inc(S(f"deviation{k}", s), 1)
                return stage

            def norm(kind, k, src, dst, free, first=0):
                def stage(i, s):
                    c = li(kind, k, i + first)
                    _, _, _, rs, nm = lns[k]
                    ready(act, f"scale{k}", s, c)
                    free(i + first, s)
                    for t in range(T):
                        a = act.activation(dst[s][:, t, :], src(s)[:, t, :], ACT.Identity, bias=nm[s][:, t:t + 1],
                                           scale=rs[s][:, t:t + 1])
                    a.then_inc(S(f"ln{k + 1}_out", s), 1)
                return stage

            def z_rows(k):
                def stage(i, s):
                    ready(act, "back", s, seq(k, i))
                    if k == 0:
                        reuse(act, "scattered", s, i, 64)
                    else:
                        reuse(act, "st_z2", s, i, 16)
                    evac(zE[s][:, :, 0:P], bBK[:, :, :], S("z_rows", s))
                return stage

            def x1_out(kind, first=0):
                def stage(i, s):
                    c = ci(kind, i + first)
                    ready(act, "x1_turned", s, c)
                    reuse(act, "hidden", s, c)
                    evac(x1T[s][:, :], flat(bIN if kind == "d" else bTR), S("x1T", s))
                return stage

            def relu(kind, first=0):
                def stage(i, s):
                    c = ci(kind, i + first)
                    ready(act, "hidden", s, c)
                    reuse(act, "mlp", s, c)
                    for h in range(HC):
                        a = act.activation(hT[h][s][:, :], flat(bH[h]), ACT.Relu, bias=b1u[:, h:h + 1])
                    a.then_inc(S("relu", s), 1)
                return stage

            def x2_out(kind, first=0):
                def stage(i, s):
                    c = ci(kind, i + first)
                    ready(act, "x2_turned", s, c)
                    reuse(act, "skip", s, c)
                    evac(x2T[s][:, :, :], bTR[:, :, :], S("x2T", s))
                return stage

            def x1_free(kind):
                def free(i, s):
                    if kind == "node":
                        reuse(act, "st_x12_", s, i, 16)
                    else:
                        at(act, "scattered", s, seq(1, i) * 64)
                    reuse(act, "x1_turned", s, ci(kind, i))
                return free

            for k in range(2):
                c = DPP * k
                steps(act, EI, (std("node", 0, c), 0),
                      (norm("node", 0, lambda s: bT1, x1, x1_free("node"), c), 0), (std("node", 3, c), 4),
                      (x2_out("node", c), 3), (relu("node", c), 1),
                      (norm("node", 3, lambda s: x3[s], x4, lambda i, s: reuse(act, "st_x4", s, i, 16), c), 4),
                      (std("node", 1, c), 2), (z_rows(k), 1), (x1_out("node", c), 0),
                      (std("node", 2, c), 3),
                      (norm("node", 2, lambda s: bSK, x3, lambda i, s: reuse(act, "st_x3_", s, i, 16), c), 3))
            all_slots(act, "st_z2", EI * 16)
            all_slots(act, "st_x3_", NI * 16)

            def x_src(i, s):
                ready(act, "turned", s, seq(3, i))
                reuse(act, "mm1", s, ci("s", i))
                evac(xT[s][:, :, :], bIN[:, :, :], S("x_src", s))

            steps(act, EI, (std("s", 0), 1), (relu("s"), 2), (x2_out("s"), 4),
                  (norm("s", 0, lambda s: bT1, x1, x1_free("s")), 1), (std("s", 1), 3), (x_src, 0), (x1_out("s"), 1), (std("s", 2), 4),
                  (norm("s", 2, lambda s: bSK, x3, lambda i, s: None), 4))

            steps(act, EI, (x1_out("d"), 0), (std("d", 1), 2), (relu("d"), 1))

            def att_src(i, s):
                ready(act, "turned", s, seq(4, i))
                reuse(act, "v_mm", s, i)
                evac(xs[s][:, :], flat(bIN), S("att_src", s))

            def att_q(i, s):
                ready(act, "q_mm", s, i)
                reuse(act, "qk", s, i)
                act.activation(qT[s][:, :], flat(bT1), ACT.Identity, bias=bqc[:, :]).then_inc(S("q_out", s), 1)

            def att_exp(i, s):
                ready(act, "delta", s, i)
                reuse(act, "agg", s, i)
                act.activation(dec[s], dlt[s], ACT.Exp).then_inc(S("decay", s), 1)
                act.activation(aw[s][:, :], elt[s], ACT.Exp).then_inc(S("weight", s), 1)

            all_slots(act, "scattered", 2 * EI * 64)
            all_slots(act, "mlp", NI + 2 * EI)
            steps(act, EI, (att_src, 0), (att_q, 0), (att_exp, 1), (std("att", 3), 4), (std("att", 2), 3),
                  (norm("att", 2, lambda s: t2[s], x3, lambda i, s: at(act, "scattered", s, seq(3, i) * 64)), 3),
                  (norm("att", 3, lambda s: x3[s], x4, lambda i, s: reuse(act, "scattered2", s, i, 64)), 4))

            steps(act, EI, (std("fin", 3), 2),
                  (norm("fin", 3, lambda s: t2[s], x4, lambda i, s: at(act, "scattered", s, seq(4, i) * 64)), 2))

        @block.vector
        def _(dve):
            dve.memset(W1a[:, :], 0.0)
            dve.memset(W1m[:, :], 0.0).then_inc(S("init_w1"), 1)
            dve.memset(zeros[:, :], 0.0).then_inc(S("init_zero"), 1)
            dve.memset(ones3[:, :], 1.0)
            dve.memset(epsc[:, :], EPS)
            dve.memset(heads[:, :], 0.0)
            dve.memset(hsel[:, :], 0.0).then_inc(S("heads0"), 1)
            dve.memset(onesE[:, :], 1.0)
            dve.wait_ge(S("heads0"), 1)
            C = P // 2
            for h in range(2):
                dve.memset(heads[h * C:(h + 1) * C, h * C:(h + 1) * C], float(C) ** -0.5)
                dve.memset(hsel[h * C:h * C + 1, h:h + 1], 1.0)
            dve.memset(ctmp[:, :], 0.0).then_inc(S("consts"), 1)
            dve.wait_ge(S("ld_flat"), 48)
            dve.tensor_copy(payl[:, :, 0], fsrc[:, :]).then_inc(S("payload"), 1)
            dve.tensor_copy(payl[:, :, 1], fdst[:, :]).then_inc(S("payload"), 1)
            dve.memset(payl[:, :, 3], 0)
            dve.tensor_copy(payl[:, :, 2].bitcast(F32), fw[:, :]).then_inc(S("payload"), 1)
            dve.wait_ge(S("ld_gsrc"), 16)
            dve.wait_ge(S("enum_i"), 2)

            def digit(k, dst, src):
                if k == 0:
                    return dve.tensor_scalar(dst, src, NB - 1, None, ALU.bitwise_and)
                return dve.tensor_scalar(dst, src, DIG, None, ALU.arith_shift_right)

            digit(0, parts_i[:, 0, 0, :], gsrc[:, :])
            digit(1, parts_i[:, 1, 0, :], gsrc[:, :])
            dve.tensor_copy(buckets[:, :], buckets_i[:, :])
            dve.drain()
            for k in range(2):
                dve.tensor_scalar(parts_i[:, k, 1, :], parts_i[:, k, 0, :], HB - 1, None, ALU.bitwise_and)
            dve.drain()
            for k in range(2):
                dve.tensor_scalar(parts_i[:, k, 0, :], parts_i[:, k, 0, :], HB.bit_length() - 1, None,
                                  ALU.arith_shift_right)
            dve.drain()
            for k in range(2):
                dve.tensor_copy(parts_a[:, :, k], parts_i[:, k, 0, :])
                dve.tensor_copy(parts_b[:, :, k], parts_i[:, k, 1, :])
            dve.drain()

            dve.wait_ge(S("ld_prep"), 80)
            dve.tensor_tensor(same[:, :], dstc[:, :], dstp[:, :], ALU.is_equal).then_inc(S("prep"), 1)
            dve.tensor_tensor(notlast[:, :], dstc[:, :], dstn[:, :], ALU.is_equal)
            dve.tensor_tensor(last[:, :], dstc[:, :], dstn[:, :], ALU.not_equal)
            dve.tensor_tensor(geq[:, :], gdst[:, :], gdn[:, :], ALU.is_equal)
            dve.drain()
            dve.tensor_scalar(samem[:, :], same[:, :], 0.5, FMAX, ALU.subtract, ALU.mult).then_inc(S("prep"), 1)
            dve.wait_ge(S("prep"), 2)
            dve.tensor_scalar(samem[:, :], samem[:, :], 2.0, None, ALU.mult).then_inc(S("flags"), 1)
            dve.tensor_scalar(ctmp[:, :], geq[:, :], float(BIG), None, ALU.mult)
            dve.tensor_scalar(ctmp2[:, :], gdst[:, :], 3.0, None, ALU.mult)
            dve.drain()
            dve.tensor_tensor(tabs["d_out"][:, :], ctmp[:, :], gdst[:, :], ALU.add).then_inc(S("d_tabs"), 1)
            dve.tensor_copy(tabs["d_x1"][:, :], ctmp2[:, :]).then_inc(S("d_tabs"), 1)
            dve.tensor_scalar(tabs["d_x2s"][:, :], gsrc[:, :], 3.0, 1.0, ALU.mult, ALU.add).then_inc(S("d_tabs"), 1)
            dve.tensor_tensor(ctmp[:, :], ctmp[:, :], ctmp2[:, :], ALU.add).then_inc(S("d_tabs"), 1)
            dve.drain()
            dve.tensor_scalar(tabs["d_x2_out"][:, :], ctmp[:, :], 1.0, None, ALU.add).then_inc(S("d_tabs"), 1)
            dve.tensor_scalar(tabs["d_x3_out"][:, :], ctmp[:, :], 2.0, None, ALU.add).then_inc(S("d_tabs"), 1)
            dve.tensor_copy(enum[:, :], enum_i[:, :]).then_inc(S("enum"), 1)
            dve.tensor_tensor_scan(cntl[:, :], same[:, :], onesE[:, :], 0.0, ALU.mult, ALU.add
                                   ).then_inc(S("cnt_local"), 1)
            dve.drain()
            dve.memset(ctmp[:, :], 0.0)
            dve.drain()
            dve.tensor_tensor_scan(allsame[:, :], same[:, :], ctmp[:, :], 1.0, ALU.mult, ALU.add
                                   ).then_inc(S("cnt_local"), 1)
            dve.wait_ge(S("carry_row"), 16)
            dve.tensor_tensor_scan(crow[:, 2, :], crow[:, 1, :], crow[:, 0, :], 0.0, ALU.mult, ALU.add
                                   ).then_inc(S("carry_scan"), 1)
            dve.wait_ge(S("carry_col"), 16)
            dve.scalar_tensor_tensor(out=ctmp[:, :], in0=allsame[:, :], scalar=ccol[:, 0:1], in1=cntl[:, :],
                                     op0=ALU.mult, op1=ALU.add).then_inc(S("prep"), 1)
            dve.wait_ge(S("prep"), 3)
            dve.reciprocal(inv[:, :], ctmp[:, :]).then_inc(S("inv"), 1)
            dve.wait_ge(S("ld_const"), 16 * 19)
            dve.wait_ge(S("ident"), 1)
            dve.tensor_tensor(W0I[:, 0, :], W0I[:, 0, :], ident[:, :], ALU.add).then_inc(S("W_ready"), 1)
            dve.tensor_tensor(WsI[:, :], WsI[:, :], ident[:, :], ALU.add).then_inc(S("W_ready"), 1)
            left = brow
            for k in range(3):
                dve.tensor_copy(bsp[:, k, :, :], left[:, :, :]).then_inc(S("bias_split"), 1)
                if k < 2:
                    dve.wait_ge(S("bias_split"), k + 1)
                    nxt = [bres, bres2][k]
                    dve.tensor_tensor(nxt[:, :, :], left[:, :, :], bsp[:, k, :, :], ALU.subtract
                                      ).then_inc(S("prep"), 1)
                    dve.wait_ge(S("prep"), k + 4)
                    left = nxt
            def parts_hot(i, s):
                reuse(dve, "counted", s, i)
                for o, parts, width in ((oha, parts_a, HA), (ohb, parts_b, HB)):
                    mine = parts[:, bass.ds((i * SL + s) * T, T), :].rearrange("p t (k a) -> p (t k) a", a=1)
                    a = dve.tensor_tensor(o[s][:, :, :, :].rearrange("p t k a -> p (t k) a"),
                                          mine.to_broadcast([P, 2 * T, width]),
                                          buckets[:, 0:width].rearrange("p (o a) -> p o a", o=1
                                                                        ).to_broadcast([P, 2 * T, width]),
                                          ALU.is_equal)
                a.then_inc(S("parts_hot"), 1)

            steps(dve, EI, (parts_hot, 0))
            all_slots(dve, "counted", EI)
            dve.tensor_copy(hist_s[:, :], bT1[0:2 * HA, 0, 0:2 * HB]).then_inc(S("hist"), 1)
            dve.wait_ge(S("ld_hist"), 16)
            for k in range(2):
                dve.tensor_tensor_scan(hscan[:, k, :], hist[:, k, :], hzero[:, :], 0.0, ALU.add, ALU.add)
            dve.drain()
            for k in range(2):
                dve.tensor_tensor(base[:, k, :], hscan[:, k, :], hist[:, k, :], ALU.subtract).then_inc(S("bases"), 1)

            for k in (1, 2):
                pair = (bH0, bH1) if k == 1 else (bMLP, bSK)

                def one_hot(i, s, j):
                    tiles_done(dve, "before", tile_no(k - 1, i, s, j - 1))
                    dve.tensor_scalar(oh[j][:, :], buckets[:, :], dig4[s][:, j:j + 1], None,
                                      ALU.is_equal).then_inc(S("one_hot"), 1)

                def digits(i, s):
                    at(dve, "ld_pay", s, (i + ((k - 1) * EI + 1)) * 16)
                    digit(k - 1, dig4i[s][:, :], pay[s][:, :, 0])
                    dve.drain()
                    dve.tensor_copy(dig4[s][:, :], dig4i[s][:, :])
                    dve.drain()
                    if isinstance(i, int) and i + s == 0:
                        one_hot(0, 0, 0)

                def rank(i, s):
                    for j in range(T):
                        if j + 1 < T:
                            one_hot(i, s, j + 1)
                        elif s + 1 < SL:
                            one_hot(i, s + 1, 0)
                        elif not isinstance(i, int) or i < EI - 1:
                            one_hot(i + 1, 0, 0)
                        tiles_done(dve, "before", tile_no(k - 1, i, s, j + 1))
                        dve.scalar_tensor_tensor(out=junk[j % 2][:, :], in0=flat(pair[j % 2]), scalar=1.0,
                                                 in1=oh[j][:, :], op0=ALU.mult, op1=ALU.mult,
                                                 accum_out=pos4[s][:, j:j + 1]).then_inc(S("ranked_tile"), 1)
                    dve.wait_ge(S("ranked_tile"), tile_no(k - 1, i, s, T))
                    at(dve, "placed", s, (i + (k - 1) * EI) * 64)
                    dve.tensor_scalar(idx[s][:, :], pos4[s][:, :], 1.0, None, ALU.add).then_inc(S("ranked", s), 1)

                steps(dve, EI, (digits, 0), (rank, 1))

            dve.wait_ge(S("ld_blocks"), 48)
            dve.tensor_tensor(bsame[:, :, :], pb[1][:, :, :, 0], pb[0][:, :, :, 0], ALU.is_equal
                              ).then_inc(S("s_rows"), 1)
            dve.tensor_copy(bw[:, :, :], pb[1][:, :, :, 2].bitcast(F32)).then_inc(S("s_rows"), 1)
            dve.tensor_copy(bsrc[:, :, :], pb[1][:, :, :, 0]).then_inc(S("blocks"), 1)
            dve.tensor_copy(bdst[:, :, :], pb[1][:, :, :, 1]).then_inc(S("blocks"), 1)
            dve.tensor_tensor(bout[:, :, :], pb[1][:, :, :, 0], pb[2][:, :, :, 0], ALU.is_equal)
            dve.drain()
            dve.scalar_tensor_tensor(out=bout[:, :, :], in0=bout[:, :, :], scalar=float(BIG), in1=pb[1][:, :, :, 0],
                                     op0=ALU.mult, op1=ALU.add).then_inc(S("blocks"), 1)
            dve.wait_ge(S("s_turned"), 3)
            tsrc, tdst, tout = (flat(b)[:, 0:EC] for b in (bH0, bH1, bMLP))
            dve.tensor_copy(tabs["s_dst"][:, :], tdst).then_inc(S("s_tabs"), 1)
            dve.tensor_copy(tabs["s_src"][:, :], tsrc).then_inc(S("s_tabs"), 1)
            dve.tensor_copy(tabs["s_out"][:, :], tout).then_inc(S("s_tabs"), 1)
            dve.tensor_scalar(tabs["s_x3d"][:, :], tdst, 3.0, 2.0, ALU.mult, ALU.add).then_inc(S("s_tabs"), 1)
            dve.tensor_scalar(tabs["s_x3s"][:, :], tsrc, 3.0, 2.0, ALU.mult, ALU.add).then_inc(S("s_tabs"), 1)

            prepared(dve)
            for s in range(SL):
                dve.memset(zE[s][:, :, :], 0.0)
            dve.memset(zT[SL - 1][:, :], 0.0).then_inc(S("carry0"), 1)
            dve.wait_ge(S("carry0"), 1)
            dve.wait_ge(S("enum"), 1)

            def stats(k, s, src):
                st, mv, _, _, _ = lns[k]
                for t in range(T):
                    dve.bn_stats(st[s][:, t, :], src[:, t, :])
                dve.drain()
                for t in range(T):
                    a = dve.bn_aggr(mv[s][:, t, :], st[s][:, t, :])
                a.then_inc(S(f"variance{k}", s), 1)

            def scale(kind, k, first=0):
                def stage(i, s):
                    c = li(kind, k, i + first)
                    _, mv, sd, rs, nm = lns[k]
                    ready(dve, f"deviation{k}", s, c)
                    reuse(dve, f"ln{k + 1}_out", s, c)
                    dve.reciprocal(rs[s][:, :], sd[s][:, :])
                    dve.drain()
                    if alone(kind, k):
                        dve.tensor_scalar(rs[s][:, :], rs[s][:, :], 1.25, None, ALU.mult)
                        dve.drain()
                    dve.scalar_tensor_tensor(out=nm[s][:, :], in0=mv[s][:, :, 0], scalar=-1.0, in1=rs[s][:, :],
                                             op0=ALU.mult, op1=ALU.mult).then_inc(S(f"scale{k}", s), 1)
                return stage

            def norm(kind, k, src, dst, free, first=0):
                def stage(i, s):
                    c = li(kind, k, i + first)
                    _, mv, sd, rs, _ = lns[k]
                    ready(dve, f"deviation{k}", s, c)
                    dve.reciprocal(rs[s][:, :], sd[s][:, :])
                    dve.drain()
                    free(i + first, s)
                    for t in range(T):
                        a = dve.tensor_scalar(dst[s][:, t, :], src[s][:, t, :], mv[s][:, t, 0:1], rs[s][:, t:t + 1],
                                              ALU.subtract, ALU.mult)
                    a.then_inc(S(f"ln{k + 1}_out", s), 1)
                return stage

            def z_weigh(k):
                def stage(i, s):
                    c = seq(k, i)
                    ready(dve, "turned", s, seq(5 if k == 3 else k, i))
                    ready(dve, "ld_row", s, c, 16)
                    dve.tensor_tensor(msg[s][:, :], flat(bIN), wB[s][:, :], ALU.mult).then_inc(S("weighted", s), 1)
                    if k == 1:
                        dve.tensor_copy(codes[:, bass.ds((i * SL + s) * T, T)], gat[s][:, :, P]
                                        ).then_inc(S("coded", s), 1)
                return stage

            def z_scan(k):
                def stage(i, s):
                    c = seq(k, i)
                    if k < 3:
                        reuse(dve, "st_zT", s, c, 16)
                    if k != 2:
                        at(dve, "back", s, i + (k if k < 2 else 2) * EI)
                    ready(dve, "weighted", s, c)
                    prior(dve, "scanned", s, c)
                    dve.tensor_tensor_scan(zT[s][:, :], fB[s][:, :], msg[s][:, :], zT[s - 1][:, G - 1:G],
                                           ALU.mult, ALU.add).then_inc(S("scanned", s), 1)
                    if k == 0:
                        reuse(dve, "scattered", s, i, 64)
                        dve.tensor_copy(zE[s][:, :, P], enum[:, bass.ds((i * SL + s) * T, T)]
                                        ).then_inc(S("numbered", s), 1)
                return stage

            def stats1(kind, first=0):
                def stage(i, s):
                    ready(dve, "mm1", s, ci(kind, i + first))
                    stats(0, s, bT1)
                return stage

            def layer2(kind, first=0):
                def stage(i, s):
                    c = ci(kind, i + first)
                    ready(dve, "mlp", s, c)
                    rows = gat[s][:, :, 0:P] if kind == "d" else x1[s]
                    dve.scalar_tensor_tensor(out=t2[s][:, :, :], in0=rows, scalar=2.0, in1=bMLP[:, :, :],
                                             op0=ALU.mult, op1=ALU.add).then_inc(S("t2", s), 1)
                    ready(dve, "t2", s, c)
                    stats(1, s, t2[s])
                return stage

            def x2_free(kind):
                def free(i, s):
                    if kind == "node":
                        reuse(dve, "st_x12_", s, i, 16)
                    if kind == "d":
                        at(dve, "scattered", s, seq(2, i) * 64)
                return free

            def stats3(kind, first=0):
                def stage(i, s):
                    ready(dve, "skip", s, ci(kind, i + first))
                    stats(2, s, bSK)
                return stage

            def stats4(kind, first=0):
                def stage(i, s):
                    ready(dve, "ln3_out", s, li(kind, 2, i + first))
                    stats(3, s, x3[s])
                return stage

            for k in range(2):
                c = DPP * k
                steps(dve, EI, (stats1("node", c), 0), (norm("node", 1, t2, x2, x2_free("node"), c), 3),
                      (scale("node", 0, c), 0), (stats4("node", c), 4), (z_weigh(k), 1), (z_scan(k), 1),
                      (scale("node", 3, c), 4), (layer2("node", c), 2), (stats3("node", c), 3),
                      (scale("node", 2, c), 3))

            all_slots(dve, "coded", EI)
            all_slots(dve, "st_x12_", NI * 16)
            all_slots(dve, "st_x4", NI * 16)
            all_slots(dve, "ln4_out", NI)
            dve.tensor_copy(tabs["s_z"][:, :], codes[:, :]).then_inc(S("s_ztab"), 1)
            for s in range(SL):
                dve.memset(att[s][:, :], 0.0)
            dve.drain()

            def attr_scan(i, s):
                ready(dve, "ld_attr", s, i, 64)
                reuse(dve, "st_att", s, i, 32)
                prior(dve, "attr_sums", s, i)
                dve.tensor_tensor_scan(att[s][0:AF, :], f2B[s][0:AF, :], atr[s][0:AF, :],
                                       att[s - 1][0:AF, G - 1:G], ALU.mult, ALU.add)
                dve.tensor_tensor_scan(att[s][AM:AK, :], fmB[s][AM:AK, :], atr[s][AM:AK, :],
                                       att[s - 1][AM:AK, G - 1:G], ALU.min, ALU.max).then_inc(S("attr_sums", s), 1)

            def attr_mean(i, s):
                ready(dve, "attr_sums", s, i)
                dve.tensor_tensor(mnt[s][0:AF, :], att[s][0:AF, :], invB[s][0:AF, :], ALU.mult
                                  ).then_inc(S("attr_mean", s), 1)

            steps(dve, EI, (attr_scan, 0), (z_weigh(2), 0), (attr_mean, 0), (z_scan(2), 0))

            steps(dve, EI, (stats1("s"), 1), (norm("s", 1, t2, x2, x2_free("s")), 4), (scale("s", 0), 1),
                  (layer2("s"), 3), (stats3("s"), 4), (scale("s", 2), 4))
            all_slots(dve, "scattered", 2 * EI * 64)
            all_slots(dve, "st_zT", 3 * EI * 16)
            dve.memset(x2d[SL - 1][:, :], 0.0).then_inc(S("carry0"), 1)
            dve.wait_ge(S("carry0"), 2)

            def x2_select(i, s):
                ready(dve, "x2_turned", s, ci("d", i))
                ready(dve, "ld_last", s, i, 16)
                dve.tensor_tensor(msg[s][:, :], flat(bTR), f2B[s][:, :], ALU.mult).then_inc(S("x2sel", s), 1)

            def x2_carry(i, s):
                reuse(dve, "st_x2d", s, i, 16)
                ready(dve, "x2sel", s, i)
                prior(dve, "x2d", s, i)
                dve.tensor_tensor_scan(x2d[s][:, ::-1], fmB[s][:, ::-1], msg[s][:, ::-1], x2d[s - 1][:, 0:1],
                                       ALU.mult, ALU.add).then_inc(S("x2d", s), 1)

            steps(dve, EI, (x2_select, 3), (layer2("d"), 2), (x2_carry, 3), (norm("d", 1, t2, x2, x2_free("d")), 2))

            def att_scores(i, s):
                ready(dve, "k_mm", s, i)
                ready(dve, "q_out", s, i)
                reuse(dve, "alpha", s, i)
                dve.scalar_tensor_tensor(out=prod[s][:, :], in0=flat(bMLP), scalar=bkc[:, 0:1], in1=qT[s][:, :],
                                         op0=ALU.add, op1=ALU.mult).then_inc(S("qk", s), 1)

            def att_max(i, s):
                ready(dve, "alpha", s, i)
                ready(dve, "ld_x2d", s, i, 32)
                prior(dve, "maxed", s, i)
                reuse(dve, "decayed", s, i)
                dve.tensor_tensor_scan(mbuf[s][:, 1:G + 1], fmB[s][:, :], flat(bSK), mbuf[s - 1][:, G:G + 1],
                                       ALU.min, ALU.max)
                dve.tensor_copy(mbuf[s][:, 0:1], mbuf[s - 1][:, G:G + 1]).then_inc(S("maxed", s), 1)
                ready(dve, "maxed", s, i)
                reuse(dve, "decay", s, i)
                dve.tensor_tensor(dlt[s], fmB[s][:, :], mbuf[s][:, 0:G], ALU.min).then_inc(S("decayed", s), 1)
                reuse(dve, "weight", s, i)
                dve.tensor_tensor(elt[s], flat(bSK), mbuf[s][:, 1:G + 1], ALU.subtract).then_inc(S("centred", s), 1)
                ready(dve, "decayed", s, i)
                dve.tensor_tensor(dlt[s], dlt[s], mbuf[s][:, 1:G + 1], ALU.subtract).then_inc(S("delta", s), 1)

            def att_weigh(i, s):
                ready(dve, "weight", s, i)
                ready(dve, "v_mm", s, i)
                dve.scalar_tensor_tensor(out=av[s][:, :], in0=flat(bH0), scalar=bvc[:, 0:1], in1=aw[s][:, :],
                                         op0=ALU.add, op1=ALU.mult).then_inc(S("weighted_v", s), 1)

            def att_sum(i, s):
                ready(dve, "decay", s, i)
                reuse(dve, "agg_turned", s, i)
                prior(dve, "agg", s, i)
                dve.tensor_tensor_scan(den[s][:, :], dec[s], aw[s][:, :], den[s - 1][:, G - 1:G], ALU.mult, ALU.add)
                ready(dve, "weighted_v", s, i)
                dve.tensor_tensor_scan(agg[s][:, :], dec[s], av[s][:, :], agg[s - 1][:, G - 1:G], ALU.mult, ALU.add
                                       ).then_inc(S("agg", s), 1)

            def att_out(i, s):
                ready(dve, "agg_turned", s, i)
                dve.tensor_scalar(dmax[s][:, :], bH1[:, 0, 0:2 * T], 1e-16, None, ALU.max)
                dve.drain()
                dve.reciprocal(rden[s][:, :], dmax[s][:, :])
                dve.drain()
                C = P // 2
                dve.tensor_tensor(flat(aggn[s]).rearrange("p (h c) -> p h c", c=C),
                                  flat(bTR).rearrange("p (h c) -> p h c", c=C),
                                  rden[s][:, :].rearrange("p (h a) -> p h a", a=1).to_broadcast([P, 2 * T, C]),
                                  ALU.mult).then_inc(S("agg_norm", s), 1)
                ready(dve, "agg_norm", s, i)
                ready(dve, "skip_e", s, i)
                at(dve, "ln3_out", s, li("att", 2, i))
                dve.tensor_tensor(t2[s][:, :, :], bBK[:, :, :], aggn[s][:, :, :], ALU.add).then_inc(S("t3", s), 1)
                ready(dve, "t3", s, i)
                stats(2, s, t2[s])

            all_slots(dve, "x2d", EI)
            all_slots(dve, "scattered", 3 * EI * 64)
            all_slots(dve, "hidden", NI + 2 * EI)
            dve.memset(den[SL - 1][:, :], 0.0)
            dve.memset(mbuf[SL - 1][:, :], 0.0)
            dve.memset(agg[SL - 1][:, :], 0.0).then_inc(S("sums0"), 1)
            dve.wait_ge(S("sums0"), 1)

            steps(dve, EI, (att_max, 1), (att_weigh, 2), (att_scores, 0), (att_sum, 2), (stats4("att"), 4),
                  (att_out, 3), (scale("att", 3), 4), (scale("att", 2), 3))

            all_slots(dve, "agg_turned", EI)
            all_slots(dve, "scattered2", EI * 64)
            dve.memset(zT[SL - 1][:, :], 0.0).then_inc(S("sums0"), 1)
            dve.wait_ge(S("sums0"), 2)

            def fin_scale(i, s):
                ready(dve, "gathered2", s, i, 64)
                dve.tensor_scalar(x2T[s][:, :, :], own[s][:, :, :], 1.25, None, ALU.mult
                                  ).then_inc(S("fin_scaled", s), 1)

            def fin_sum(i, s):
                ready(dve, "back", s, seq(2, i))
                ready(dve, "fin_scaled", s, i)
                at(dve, "ln4_out", s, li("fin", 3, i))
                dve.scalar_tensor_tensor(out=t2[s][:, :, :], in0=bBK[:, :, :], scalar=0.75, in1=x2T[s][:, :, :],
                                         op0=ALU.mult, op1=ALU.add).then_inc(S("fin_sum", s), 1)
                ready(dve, "fin_sum", s, i)
                stats(3, s, t2[s])

            steps(dve, EI, (z_weigh(3), 0), (fin_scale, 1), (z_scan(3), 0), (fin_sum, 2), (scale("fin", 3), 2))


def kernel(**inputs):
    import numpy as np
    import concourse.bacc as bacc
    from concourse.bass_utils import run_bass_kernel_spmd as run

    a = {k: np.asarray(v) for k, v in inputs.items()}
    N, D = a["x"].shape
    E = a["src"].shape[0]
    N_PAD = -(-(N + 1) // (2 * SL * G)) * 2 * SL * G
    E_PAD = -(-E // (SL * G)) * SL * G
    if N_PAD != 2 * E_PAD:
        N_PAD = max(N_PAD, 2 * E_PAD)
        E_PAD = N_PAD // 2

    def padded(v, n, fill):
        out = np.full((n,) + v.shape[1:], fill, v.dtype)
        out[:v.shape[0]] = v
        return out

    src = padded(a["src"], E_PAD, N_PAD - 1)
    dst = padded(a["dst"], E_PAD, N_PAD - 1)
    dst_flat = np.full((E_PAD + 2,), -1, dst.dtype)
    dst_flat[1:-1] = dst
    x_rows = padded(a["x"], N_PAD, 0)
    AF = a["edge_attr_48"].shape[1]
    attr_fm = np.zeros((AM + AF, E_PAD), np.float32)
    attr_fm[:AF, :E] = attr_fm[AM:, :E] = a["edge_attr_48"].T
    arrays = {
        "x_fm": np.ascontiguousarray(x_rows.reshape(-1, P, T, D).transpose(3, 0, 2, 1).reshape(D, N_PAD)),
        "x_rows": x_rows,
        "src_g": np.ascontiguousarray(src.reshape(-1, P).T),
        "dst_g": np.ascontiguousarray(dst.reshape(-1, P).T),
        "dnext_g": np.ascontiguousarray(dst_flat[2:].reshape(-1, P).T),
        "src_flat": src,
        "dst_flat": dst_flat,
        "w_flat": padded(a["edge_weight"], E_PAD, 0),
        "attr_fm": attr_fm,
    }
    for n in ("L0_gnn_W", "L0_gnn_b", "L1_gnn_u", "L1_gnn_W1", "L1_gnn_b1", "L1_gnn_W2", "L1_gnn_b2",
              "L2_gnn_Wq", "L2_gnn_bq", "L2_gnn_Wk", "L2_gnn_bk", "L2_gnn_Wv", "L2_gnn_bv", "L2_gnn_Wskip",
              "L2_gnn_bskip"):
        arrays[n] = np.ascontiguousarray(a[n])
    nc = bacc.Bacc("TRN2", target_bir_lowering=False, num_devices=1)
    args = [nc.dram_tensor("in_" + n, v.shape, mybir.dt.from_np(v.dtype), kind="ExternalInput").ap()
            for n, v in arrays.items()]
    out = nc.dram_tensor("out_rows", (N_PAD, D), F32, kind="ExternalOutput").ap()
    gnn_kernel(nc, *args, out)
    r = run(nc, [{"in_" + n: v for n, v in arrays.items()}], core_ids=[0])
    return r.results[0]["out_rows"][:N]
```
